# Optimizing a Trainium2 kernel written in Bass

```python
import numpy as np
import jax
import jax.numpy as jnp

def _softmax(x, axis=-1):
    return jax.nn.softmax(x, axis=axis)

def _gelu(x):
    return jax.nn.gelu(x, approximate=True)

def _silu(x):
    return jax.nn.silu(x)

def _sigmoid(x):
    return jax.nn.sigmoid(x)

def _layernorm(x, axis=-1, eps=1e-05):
    m = jnp.mean(x, axis=axis, keepdims=True)
    v = jnp.var(x, axis=axis, keepdims=True)
    return (x - m) / jnp.sqrt(v + eps)

def _scatter_add(tgt, idx, src, axis=0):
    return tgt.at[idx].add(src)

def _segment_sum(src, seg, n):
    return jax.ops.segment_sum(src, seg, n)
kernel_name = 'mk_prb_d1_jaxref_r8_8ea115'

def setup_inputs(seed: int=0):
    np.random.seed(seed)
    _w = jnp.asarray

    def _L0_attn_setup():
        import jax, jax.numpy as jnp
        import numpy as np
        N_EMBD = 128
        N_HEAD = 16
        HEAD_DIM = N_EMBD // N_HEAD
        LATENT_DIM = N_EMBD // 2
        B, T = (4, 256)
        key = jax.random.key(seed)
        ks = jax.random.split(key, 5)

        def init(k, fan_in, fan_out):
            bound = 1.0 / np.sqrt(fan_in)
            return jax.random.uniform(k, (fan_in, fan_out), jnp.float32, -bound, bound)
        return {'x': jax.random.normal(ks[0], (B, T, N_EMBD), jnp.float32), 'Wc_down': init(ks[1], N_EMBD, LATENT_DIM), 'Wq_up': init(ks[2], LATENT_DIM, N_EMBD), 'Wkv_up': init(ks[3], LATENT_DIM, 2 * HEAD_DIM), 'Wc_proj': init(ks[4], N_EMBD, N_EMBD)}
    _L0_attn_in = _L0_attn_setup()

    def _L0_ffn_setup():
        import jax, jax.numpy as jnp
        import numpy as np
        B, S, D, F, E, NS, K = (2, 128, 128, 512, 8, 8, 2)
        FS = F // NS
        key = jax.random.key(seed)
        ks = jax.random.split(key, 8)
        scale = 0.02
        return {'hidden_states': jax.random.normal(ks[0], (B, S, D), jnp.float32), 'gate_W': jax.random.normal(ks[1], (E, D), jnp.float32) * scale, 'w1_e': jax.random.normal(ks[2], (E, D, F), jnp.float32) * scale, 'w3_e': jax.random.normal(ks[3], (E, D, F), jnp.float32) * scale, 'w2_e': jax.random.normal(ks[4], (E, F, D), jnp.float32) * scale, 'w1_s': jax.random.normal(ks[5], (NS, D, FS), jnp.float32) * scale, 'w3_s': jax.random.normal(ks[6], (NS, D, FS), jnp.float32) * scale, 'w2_s': jax.random.normal(ks[7], (NS, FS, D), jnp.float32) * scale}
    _L0_ffn_in = _L0_ffn_setup()
    _d = {'L0_attn_x': _L0_attn_in['x'], 'L0_attn_Wc_down': _L0_attn_in['Wc_down'], 'L0_attn_Wq_up': _L0_attn_in['Wq_up'], 'L0_attn_Wkv_up': _L0_attn_in['Wkv_up'], 'L0_attn_Wc_proj': _L0_attn_in['Wc_proj'], 'L0_ffn_gate_W': _L0_ffn_in['gate_W'], 'L0_ffn_w1_e': _L0_ffn_in['w1_e'], 'L0_ffn_w3_e': _L0_ffn_in['w3_e'], 'L0_ffn_w2_e': _L0_ffn_in['w2_e'], 'L0_ffn_w1_s': _L0_ffn_in['w1_s'], 'L0_ffn_w3_s': _L0_ffn_in['w3_s'], 'L0_ffn_w2_s': _L0_ffn_in['w2_s']}
    _x0 = _d['L0_attn_x']
    _d['L0_attn_x'] = jax.random.normal(jax.random.fold_in(jax.random.key(seed), 1), (8, 512, 128), dtype=_x0.dtype)
    del _x0
    return _d

def reference(L0_attn_x, L0_attn_Wc_down, L0_attn_Wq_up, L0_attn_Wkv_up, L0_attn_Wc_proj, L0_ffn_gate_W, L0_ffn_w1_e, L0_ffn_w3_e, L0_ffn_w2_e, L0_ffn_w1_s, L0_ffn_w3_s, L0_ffn_w2_s):

    def _L0_attn_ref(x, Wc_down, Wq_up, Wkv_up, Wc_proj):
        import jax, jax.numpy as jnp
        import numpy as np
        N_EMBD = 128
        N_HEAD = 16
        HEAD_DIM = N_EMBD // N_HEAD
        LATENT_DIM = N_EMBD // 2
        B, T = (4, 256)
        Bsz, Tlen, C = x.shape
        latent = x @ Wc_down
        q = (latent @ Wq_up).reshape(Bsz, Tlen, N_HEAD, HEAD_DIM)
        kv = latent @ Wkv_up
        k, v = (kv[..., :HEAD_DIM], kv[..., HEAD_DIM:])
        scale = 1.0 / np.sqrt(HEAD_DIM)
        att = jnp.einsum('bthd,bsd->bhts', q, k) * scale
        causal = jnp.tril(jnp.ones((Tlen, Tlen), dtype=bool))
        att = jnp.where(causal[None, None], att, -jnp.inf)
        att = jax.nn.softmax(att, axis=-1)
        y = jnp.einsum('bhts,bsd->bthd', att, v).reshape(Bsz, Tlen, C)
        return y @ Wc_proj

    def _L0_ffn_ref(hidden_states, gate_W, w1_e, w3_e, w2_e, w1_s, w3_s, w2_s):
        import jax, jax.numpy as jnp
        import numpy as np
        B, S, D, F, E, NS, K = (2, 128, 128, 512, 8, 8, 2)
        FS = F // NS
        b, s, d = hidden_states.shape
        e = gate_W.shape[0]
        flat = hidden_states.reshape(-1, d)
        T = flat.shape[0]
        logits = (flat @ gate_W.T).astype(jnp.float32)
        probs = jax.nn.softmax(logits, axis=-1)
        top_v, top_i = jax.lax.top_k(probs, K)
        gates = jnp.zeros((T, e), probs.dtype).at[jnp.arange(T)[:, None], top_i].set(top_v)
        g = jax.nn.silu(jnp.einsum('td,edf->etf', flat, w1_e))
        u = jnp.einsum('td,edf->etf', flat, w3_e)
        out_e = jnp.einsum('etf,efd->etd', g * u, w2_e)
        routed = jnp.einsum('te,etd->td', gates, out_e).reshape(b, s, d)
        gs = jax.nn.silu(jnp.einsum('bsd,ndf->nbsf', hidden_states, w1_s))
        us = jnp.einsum('bsd,ndf->nbsf', hidden_states, w3_s)
        shared = jnp.einsum('nbsf,nfd->bsd', gs * us, w2_s) / w1_s.shape[0]
        alpha = 0.5
        return alpha * shared + (1.0 - alpha) * routed
    x = L0_attn_x
    xn = _layernorm(x, axis=-1)
    x = x + _L0_attn_ref(xn, L0_attn_Wc_down, L0_attn_Wq_up, L0_attn_Wkv_up, L0_attn_Wc_proj) + _L0_ffn_ref(xn, L0_ffn_gate_W, L0_ffn_w1_e, L0_ffn_w3_e, L0_ffn_w2_e, L0_ffn_w1_s, L0_ffn_w3_s, L0_ffn_w2_s)
    return x

_drawn_inputs = setup_inputs


def setup_inputs(seed=0):
    import zlib

    import numpy as np

    out = dict(_drawn_inputs(seed))
    spreads = {}
    factors = {'L0_attn_Wc_down': 2.803,
     'L0_attn_Wq_up': 8.0,
     'L0_attn_Wkv_up': 2.872,
     'L0_attn_Wc_proj': 2.883,
     'L0_ffn_gate_W': 8.0,
     'L0_ffn_w1_e': 8.0,
     'L0_ffn_w3_e': 8.0,
     'L0_ffn_w2_e': 8.0,
     'L0_ffn_w1_s': 8.0,
     'L0_ffn_w3_s': 8.0,
     'L0_ffn_w2_s': 8.0}
    for name, (base, spread) in spreads.items():
        noise = np.random.default_rng([zlib.crc32(name.encode()), seed]).standard_normal(out[name].shape)
        drawn = base * np.exp(spread * noise) if base else spread * noise
        out[name] = jnp.asarray(drawn.astype(out[name].dtype))
    for name, factor in factors.items():
        out[name] = (out[name] * factor).astype(out[name].dtype)
    return out
```

```python
from contextlib import ExitStack

import concourse.bass as bass
from concourse import mybir

F32 = mybir.dt.float32
BF16 = mybir.dt.bfloat16
U32 = mybir.dt.uint32
I32 = mybir.dt.int32
ALU = mybir.AluOpType
ACT = mybir.ActivationFunctionType
AX = mybir.AxisListType

P = 128
D = 128
LAT = 64
HEADS, HD = 16, 8
GROUPS = 4
HG = HEADS // GROUPS
TB = 4
T = TB * P
EXPERTS = 8
SETS = EXPERTS + 1
F = 512
FC = F // P
UNITS = SETS * FC
EPS = 1e-5
SCALE = HD ** -0.5
NEVER = -3.0e38
ROUTED = 0.5 * 0.5
SHARED = 0.5 * 0.5 / 8

PARTS = 3
STACK = PARTS * PARTS * HD
MROW = 96
STACKED = MROW + PARTS

PCOL = {0: 0, 1: 512, 3: 896, 2: 1024}
PCOLS = 1280

A_BANKS = [(3, 0, 1), (3, 1, 1), (3, 2, 1), (3, 3, 1), (2, 0, 1), (2, 1, 1), (2, 2, 1), (2, 3, 1),
           (1, 0, 2), (1, 2, 2), (0, 0, 4)]
B_BANKS = [(h, 1, (0,)) for h in range(HG)] + [(h, 1, (1, 3)) for h in range(HG)] + [(0, 2, (2,)), (2, 2, (2,))]
NA, NB = len(A_BANKS), len(B_BANKS)
RING = 3
A_ALL, B_ALL = GROUPS * NA, GROUPS * NB

STEPS = 3 * UNITS


def plan(prepare):
    at = [[] for _ in range(STEPS + 1)]
    at[0] += [("latent",)]
    at[2] += [("query",)]
    at[4] += [("keys",)]
    at[9] += [("kstack",)]
    for g in range(GROUPS):
        for i in range(NA):
            at[16 + NA * g + i] += [("a", g, i)]
        at[29 + NA * g] += [("maxima", g)]
        for i in range(NB):
            at[37 + NA * g + i] += [("b", g, i)]
        at[51 + NA * g] += [("pv", g)]
        at[54 + NA * g] += [("heads", g)]
    at[92] += [("turn",)]
    at[96] += [("project",)]
    for e in range(1, SETS):
        at[12 * (e - 1) + 5] += [("gate", e)]
    if prepare:
        at[58] += [("norm",)]
        at[66] += [("xt",)]
        at[74] += [("logits",)]
        at[80] += [("route",)]
        at[99] += [("gates",)]
    at[STEPS] += [("out",)]
    return at


MISC = ("latent", "query", "keys", "kstack", "maxima", "heads", "turn", "gate", "xt", "logits", "gates", "out")
PREPARE = [("norm",), ("xt",), ("logits",), ("route",), ("gates",)]


def places(items, kinds):
    return {item: n for n, item in enumerate(i for i in items if i[0] in kinds)}


def sequences(eng, run, B):
    run(0, True)
    with eng.Fori(1, B - 1) as b:
        run(b, True)
    run(B - 1, False)


def build(nc, x, Wc_down, Wq_up, Wkv_up, Wc_proj, gate_W, w1_e, w3_e, w2_e, w1_s, w3_s, w2_s, out):
    B = x.shape[0]
    flat = {prep: [i for step in plan(prep) for i in step] for prep in (True, False)}
    misc_at = {prep: places(flat[prep], MISC) for prep in flat}
    MISC_PER = len(misc_at[True])
    MISC_BEFORE = len([i for i in PREPARE if i[0] in MISC])
    ring_at = {prep: places(flat[prep], ("a", "b")) for prep in flat}
    ring_items = [i for i in flat[True] if i[0] in ("a", "b")]
    assert ring_at[True] == ring_at[False] and len(ring_items) % RING == 0

    with ExitStack() as ctx:
        def sb(name, shape, dt=F32):
            return ctx.enter_context(nc.sbuf_tensor(name, shape, dt))

        def bank(name, shape):
            return ctx.enter_context(nc.psum_tensor(name, shape, F32))

        def sem(name):
            return ctx.enter_context(nc.semaphore(name))

        ring = bank("ring", [P, RING, 512])
        pvb = bank("pvb", [P, 512])
        gb = bank("gb", [P, 512])
        ub = bank("ub", [P, 512])
        acc = bank("acc", [P, 512])
        misc = bank("misc", [P, 512])
        misc16 = misc[:].bitcast(BF16)

        w1 = sb("w1", [P, SETS, F])
        w3 = sb("w3", [P, SETS, F])
        w2 = sb("w2", [P, SETS, FC, D])
        wdown = sb("wdown", [P, P])
        wq = sb("wq", [P, P])
        wkv = sb("wkv", [P, 2 * HD])
        wproj = sb("wproj", [P, D])
        gw = sb("gw", [EXPERTS, D])
        gwT = sb("gwT", [P, EXPERTS])
        ident = sb("ident", [P, P])
        ident16 = sb("ident16", [P, P], BF16)
        never = sb("never", [P, P], BF16)
        pick = sb("pick", [96, EXPERTS, P], BF16)
        number_i = sb("number_i", [P, EXPERTS], I32)
        number = sb("number", [P, EXPERTS])
        minus_half = sb("minus_half", [P, TB])
        xt = sb("xt", [P, TB, D])
        stats = sb("stats", [P, TB, 6])
        meanvar = sb("meanvar", [P, TB, 2])
        vareps = sb("vareps", [P, TB])
        rstd = sb("rstd", [P, TB])
        xn = sb("xn", [P, TB, D])
        xnT_next = sb("xnT_next", [P, T])
        xnT = sb("xnT", [P, T])
        lmax = sb("lmax", [P, TB])
        lshift = sb("lshift", [P, TB * EXPERTS])
        lexp = sb("lexp", [P, TB * EXPERTS])
        lsum = sb("lsum", [P, TB])
        linv = sb("linv", [P, TB])
        probs = sb("probs", [P, TB * EXPERTS])
        top = sb("top", [P, TB, 8])
        topi = sb("topi", [P, TB, 8], U32)
        topf = sb("topf", [P, TB, 8])
        first = sb("first", [P, TB * EXPERTS])
        second = sb("second", [P, TB * EXPERTS])
        gates = sb("gates", [P, TB * EXPERTS])
        gleft = sb("gleft", [P, TB * EXPERTS])
        gparts = sb("gparts", [P, TB, 96], BF16)
        gpartsT = sb("gpartsT", [96, T], BF16)
        latT = sb("latT", [P, T])
        qparts = sb("qparts", [P, PARTS, T], BF16)
        qleft = sb("qleft", [P, T])
        qst = sb("qst", [P, HEADS, T], BF16)
        kleft = sb("kleft", [P, TB, HD])
        krows = sb("krows", [P, TB, P], BF16)
        kst = sb("kst", [P, T], BF16)
        vaug = sb("vaug", [P, TB, 32])
        nmax = sb("nmax", [P, TB, HEADS])
        mleft = sb("mleft", [P, TB, HG])
        mparts = sb("mparts", [P, TB, PARTS, HG], BF16)
        mT = sb("mT", [PARTS * HG, T], BF16)
        probT = sb("probT", [P, 2, HG, PCOLS])
        hraw = sb("hraw", [P, T])
        dinv = sb("dinv", [P, TB * HG])
        y = sb("y", [P, TB, D])
        yT = sb("yT", [P, T])
        xe = sb("xe", [P, 2, T])
        th = sb("th", [P, 2, T])
        ga = sb("ga", [P, T])
        hid = sb("hid", [P, 2, T])
        accs = sb("accs", [P, T])
        xres = sb("xres", [P, TB, D])
        res = sb("res", [P, TB, D])
        q_dram = nc.dram_tensor("q_scratch", (PARTS, HEADS, HD, T), BF16, kind="Internal").ap()
        m_dram = nc.dram_tensor("m_scratch", (GROUPS, PARTS, HG, T), BF16, kind="Internal").ap()

        s_w = [sem(f"weights_loaded_{e}") for e in range(SETS)]
        s_small = sem("small_weights_loaded")
        s_zero = sem("buffers_zeroed")
        s_const = sem("constants_made")
        s_gwT = sem("gate_weights_turned")
        s_gwTs = sem("gate_weights_saved")
        s_xt = sem("x_loaded")
        s_vareps = sem("variance_ready")
        s_rstd = sem("rstd_ready")
        s_norm = sem("normed")
        s_next = sem("xnT_next_ready")
        s_xnT = sem("xnT_ready")
        s_lshift = sem("logits_shifted")
        s_lexp = sem("logits_exped")
        s_gparts = sem("gate_parts_ready")
        s_gT = sem("gate_parts_turned")
        s_lat = sem("latent_ready")
        s_q1 = sem("query_first_part")
        s_q = sem("query_parts_ready")
        s_qst0 = sem("query_parts_stored")
        s_qst = sem("query_stack_loaded")
        s_krows = sem("key_rows_ready")
        s_kst = sem("key_stack_ready")
        s_a = sem("a_scored")
        s_amax = sem("a_maxed")
        s_mparts = sem("maxima_parts_ready")
        s_mT = sem("maxima_turned")
        s_mst = sem("maxima_stored")
        s_m = [sem(f"maxima_loaded_{g}") for g in range(GROUPS)]
        s_b = sem("b_scored")
        s_exp = sem("b_exped")
        s_pv = sem("heads_summed")
        s_hraw = sem("heads_saved")
        s_y = sem("heads_normed")
        s_yT = sem("yT_ready")
        s_misc = sem("misc_filled")
        s_free = sem("misc_read")
        s_xe = sem("gated_x_ready")
        s_g = sem("g_ready")
        s_th = sem("tanh_done")
        s_gfree = sem("g_read")
        s_u = sem("u_ready")
        s_h = sem("hidden_ready")
        s_down = sem("down_done")
        s_acc = sem("acc_ready")
        s_accs = sem("acc_saved")
        s_xres = sem("x_again_loaded")
        s_res = sem("result_ready")
        s_out = sem("result_stored")
        s_dve = sem("vector_step")
        s_apart = sem("waits_carried")

        def misc_use(b, prep, item):
            if b is None:
                return places(PREPARE, MISC)[item]
            return MISC_BEFORE + b * MISC_PER + misc_at[prep][item]

        def scores_out(item):
            return ring[:, ring_at[True][item] % RING, :]

        block = ctx.enter_context(nc.Block())

        @block.sync
        def _(sp):
            x_tiles = x.rearrange("b (t p) d -> b p t d", p=P)
            out_tiles = out.rearrange("b (t p) d -> b p t d", p=P)
            sp.dma_start(xt[:], x_tiles[0]).then_inc(s_xt, 16)
            sp.dma_start(gw[:], gate_W).then_inc(s_small, 16)
            sp.wait_ge(s_zero, 1)
            sp.dma_start(wdown[:, 0:LAT], Wc_down).then_inc(s_small, 16)
            sp.dma_start(wq[0:LAT, :], Wq_up).then_inc(s_small, 16)
            sp.dma_start(wkv[0:LAT, :], Wkv_up).then_inc(s_small, 16)
            sp.dma_start(wproj[:], Wc_proj).then_inc(s_small, 16)
            for e in range(1, SETS):
                sp.dma_start(w1[:, e, :], w1_e[e - 1]).then_inc(s_w[e], 16)
                sp.dma_start(w3[:, e, :], w3_e[e - 1]).then_inc(s_w[e], 16)
                sp.dma_start(w2[:, e, :, :], w2_e[e - 1].rearrange("(c p) d -> p c d", p=P)).then_inc(s_w[e], 16)

            def sequence(b, prep):
                sp.wait_ge(s_res, b)
                sp.sem_inc(s_apart, 1)
                sp.dma_start(xres[:], x_tiles[b]).then_inc(s_xres, 16)
                if prep:
                    sp.wait_ge(s_norm, b + 1)
                    sp.sem_inc(s_apart, 1)
                    sp.dma_start(xt[:], x_tiles[b + 1]).then_inc(s_xt, 16)
                sp.wait_ge(s_q, b + 1)
                sp.sem_inc(s_apart, 1)
                sp.wait_ge(s_qst, b * 16 * PARTS * PARTS)
                sp.sem_inc(s_apart, 1)
                sp.dma_start(q_dram.rearrange("i h d t -> (h d) i t"), qparts[:]).then_inc(s_qst0, 16)
                sp.wait_ge(s_qst0, 16 * (b + 1))
                sp.sem_inc(s_apart, 1)
                sp.wait_ge(s_b, B_ALL * b)
                sp.sem_inc(s_apart, 1)
                for i in range(PARTS):
                    for j in range(PARTS):
                        row = (i * PARTS + j) * HD
                        sp.dma_start(qst[row:row + HD, :, :], q_dram[i].rearrange("h d t -> d h t")).then_inc(s_qst, 16)
                for g in range(GROUPS):
                    sp.wait_ge(s_mT, GROUPS * b + g + 1)
                    sp.sem_inc(s_apart, 1)
                    sp.dma_start(m_dram[g].rearrange("i h t -> (i h) t"), mT[:]).then_inc(s_mst, 16)
                    sp.wait_ge(s_mst, 16 * (GROUPS * b + g + 1))
                    sp.sem_inc(s_apart, 1)
                    sp.dma_start(qst[MROW:STACKED, HG * g:HG * g + HG, :], m_dram[g]).then_inc(s_m[g], 16)
                sp.wait_ge(s_res, b + 1)
                sp.sem_inc(s_apart, 1)
                sp.dma_start(out_tiles[b], res[:]).then_inc(s_out, 16)

            sequences(sp, sequence, B)
            sp.wait_ge(s_out, 16 * B)

        @block.tensor
        def _(pe):
            def take_misc(b, prep, item):
                n = misc_use(b, prep, item)
                pe.wait_ge(s_free, n)

            def transposes(b, prep, item, of, eye, where):
                for t in range(TB):
                    last = nc.tensor.transpose(where(t), of(t), eye)
                last.then_inc(s_misc, 1)

            def do(b, prep, item):
                kind = item[0]
                n = 0 if b is None else b
                if kind in MISC:
                    take_misc(b, prep, item)
                if kind == "xt":
                    pe.wait_ge(s_norm, 1 if b is None else b + 2)
                    transposes(b, prep, item, lambda t: xn[:, t, :], ident[:], lambda t: misc[:, t * P:(t + 1) * P])
                elif kind == "logits":
                    pe.wait_ge(s_next, 1 if b is None else b + 2)
                    for t in range(TB):
                        last = nc.tensor.matmul(misc[:, t * EXPERTS:(t + 1) * EXPERTS],
                                                xnT_next[:, t * P:(t + 1) * P], gwT[:], start=(t == 0), stop=True,
                                                skip_group_check=True)
                    last.then_inc(s_misc, 1)
                elif kind == "gates":
                    pe.wait_ge(s_gparts, 1 if b is None else b + 2)
                    transposes(b, prep, item, lambda t: gparts[:, t, :], ident16[:],
                               lambda t: misc16[0:96, t * P:(t + 1) * P])
                elif kind == "latent":
                    pe.wait_ge(s_xnT, b + 1)
                    nc.tensor.matmul(misc[:], wdown[:], xnT[:], start=True, stop=True).then_inc(s_misc, 1)
                elif kind == "query":
                    pe.wait_ge(s_lat, b + 1)
                    nc.tensor.matmul(misc[:], wq[:], latT[:], start=True, stop=True).then_inc(s_misc, 1)
                elif kind == "keys":
                    for t in range(TB):
                        last = nc.tensor.matmul(misc[:, t * 2 * HD:(t + 1) * 2 * HD], latT[:, t * P:(t + 1) * P],
                                                wkv[:], start=(t == 0), stop=True, skip_group_check=True)
                    last.then_inc(s_misc, 1)
                elif kind == "kstack":
                    pe.wait_ge(s_krows, b + 1)
                    transposes(b, prep, item, lambda t: krows[:, t, :], ident16[:],
                               lambda t: misc16[:, t * P:(t + 1) * P])
                elif kind == "gate":
                    e = item[1]
                    pe.wait_ge(s_gT, b + 1)
                    nc.tensor.matmul(misc[:], pick[:, e - 1, :], gpartsT[:], start=True, stop=True).then_inc(s_misc, 1)
                elif kind in ("a", "b"):
                    k = ring_at[True][item]
                    before = ring_items[k - RING]
                    past = 0 if k >= RING else 1
                    if past:
                        pe.wait_ge(s_exp, B_ALL * b)
                    elif before[0] == "a":
                        pe.wait_ge(s_amax, A_ALL * b + NA * before[1] + before[2] + 1)
                    else:
                        pe.wait_ge(s_exp, B_ALL * b + NB * before[1] + before[2] + 1)
                    if kind == "a":
                        scores_a(b, item)
                    else:
                        scores_b(b, item)
                elif kind == "maxima":
                    g = item[1]
                    pe.wait_ge(s_mparts, GROUPS * b + g + 1)
                    transposes(b, prep, item, lambda t: mparts[:, t].rearrange("p i h -> p (i h)"), ident16[:],
                               lambda t: misc16[0:PARTS * HG, t * P:(t + 1) * P])
                elif kind == "pv":
                    pv(b, item[1])
                elif kind == "heads":
                    g = item[1]
                    pe.wait_ge(s_hraw, GROUPS * b + g + 1)
                    transposes(b, prep, item, lambda t: hraw[:, t * P:(t + 1) * P], ident[:],
                               lambda t: misc[:, t * P:(t + 1) * P])
                elif kind == "turn":
                    pe.wait_ge(s_y, GROUPS * (b + 1))
                    transposes(b, prep, item, lambda t: y[:, t, :], ident[:], lambda t: misc[:, t * P:(t + 1) * P])
                elif kind == "project":
                    pe.wait_ge(s_yT, b + 1)
                    nc.tensor.matmul(acc[:], wproj[:], yT[:], start=False, stop=False, skip_group_check=True)
                elif kind == "out":
                    pe.wait_ge(s_accs, b + 1)
                    transposes(b, prep, item, lambda t: accs[:, t * P:(t + 1) * P], ident[:],
                               lambda t: misc[:, t * P:(t + 1) * P])

            def scores_a(b, item):
                _, g, i = item
                t, h0, n = A_BANKS[i]
                if (g, i) == (0, 0):
                    pe.wait_ge(s_qst, 16 * PARTS * PARTS * (b + 1))
                    pe.wait_ge(s_kst, b + 1)
                keys = (t + 1) * P
                o = scores_out(item)
                for h in range(n):
                    nc.tensor.matmul(o[:, h * keys:(h + 1) * keys], qst[0:MROW, HG * g + h0 + h, t * P:(t + 1) * P],
                                     kst[0:MROW, 0:keys], start=(h == 0), stop=False, skip_group_check=True)
                diagonal = o[:, 0:n * keys].rearrange("p (h s) -> p h s", h=n)[:, :, t * P:keys]
                nc.tensor.matmul(diagonal, ident16[:], never[:].unsqueeze(1).broadcast_to([P, n, P]), start=False,
                                 stop=True, skip_group_check=True).then_inc(s_a, 1)

            def scores_b(b, item):
                _, g, i = item
                h0, n, tiles = B_BANKS[i]
                if i == 0:
                    pe.wait_ge(s_m[g], 16 * (b + 1))
                o = scores_out(item)
                col = 0
                for h in range(h0, h0 + n):
                    for s in tiles:
                        w = T - s * P
                        nc.tensor.matmul(o[:, col:col + w], kst[0:STACKED, s * P:(s + 1) * P],
                                                qst[0:STACKED, HG * g + h, s * P:T], start=(col == 0), stop=False,
                                         skip_group_check=True)
                        col += w
                if len(tiles) * n == 1:
                    diagonal = o[:, 0:P]
                    eye = ident16[:]
                else:
                    far = T - tiles[0] * P
                    diagonal = (o.rearrange("p (c w) -> p c w", w=P)[:, 0:4:3, :] if far == 3 * P else
                                o.rearrange("p (n c) -> p n c", n=2)[:, :, 0:P])
                    eye = ident16[:].unsqueeze(1).broadcast_to([P, 2, P])
                nc.tensor.matmul(diagonal, never[:], eye, start=False, stop=True, skip_group_check=True).then_inc(s_b, 1)

            def pv(b, g):
                pe.wait_ge(s_exp, B_ALL * b + NB * (g + 1))
                pe.wait_ge(s_hraw, GROUPS * b + g)
                for s in range(TB):
                    for h in range(HG):
                        c = PCOL[s]
                        last = nc.tensor.matmul(pvb[32 * h:32 * h + 32, s * P:T], vaug[:, s, :],
                                                probT[:, g % 2, h, c:c + T - s * P], start=(s == 0),
                                                stop=(s == TB - 1), skip_group_check=True)
                last.then_inc(s_pv, 1)

            def down(b, f):
                pe.wait_ge(s_h, UNITS * b + f + 1)
                if f == 0:
                    pe.wait_ge(s_accs, b)
                mm = nc.tensor.matmul(acc[:], w2[:, f // FC, f % FC, :], hid[:, f % 2, :], start=(f == 0),
                                      stop=(f == UNITS - 1), skip_group_check=True)
                mm.then_inc(s_down, 1)
                if f == UNITS - 1:
                    pass

            def sequence(b, prep):
                steps = plan(prep)
                for step in range(STEPS):
                    f, k = divmod(step, 3)
                    e, c = divmod(f, FC)
                    for item in steps[step]:
                        do(b, prep, item)
                    if k == 0:
                        if f == 0:
                            pe.wait_ge(s_xnT, b + 1)
                        if c == 0:
                            pe.wait_ge(s_w[e], 48)
                        pe.wait_ge(s_gfree, UNITS * b + f)
                        nc.tensor.matmul(gb[:], w1[:, e, c * P:(c + 1) * P], xnT[:], start=True,
                                         stop=True).then_inc(s_g, 1)
                    elif k == 1:
                        if c == 0:
                            pe.wait_ge(s_xe, SETS * b + e + 1)
                        pe.wait_ge(s_h, UNITS * b + f)
                        nc.tensor.matmul(ub[:], w3[:, e, c * P:(c + 1) * P], xe[:, e % 2, :], start=True,
                                         stop=True).then_inc(s_u, 1)
                    elif f:
                        down(b, f - 1)
                down(b, UNITS - 1)
                for item in steps[STEPS]:
                    do(b, prep, item)

            pe.wait_ge(s_const, 1)
            pe.wait_ge(s_small, 16 * 5)
            nc.tensor.transpose(acc[:, 0:EXPERTS], gw[:], ident[0:EXPERTS, 0:EXPERTS]).then_inc(s_gwT, 1)
            pe.wait_ge(s_gwTs, 1)
            for item in PREPARE:
                do(None, True, item)
            sequences(pe, sequence, B)

        @block.scalar
        def _(act):
            act.dma_start(w1[:, 0, :].rearrange("p (n f) -> p n f", n=8), w1_s.rearrange("n d f -> d n f")).then_inc(s_w[0], 16)
            act.dma_start(w3[:, 0, :].rearrange("p (n f) -> p n f", n=8), w3_s.rearrange("n d f -> d n f")).then_inc(s_w[0], 16)
            act.dma_start(w2[:, 0, :, :], w2_s.rearrange("n f d -> (n f) d").rearrange("(c p) d -> p c d", p=P)).then_inc(s_w[0], 16)

            def filled(b, prep, item):
                act.wait_ge(s_misc, misc_use(b, prep, item) + 1)

            def do(b, prep, item):
                kind = item[0]
                if kind == "xt":
                    filled(b, prep, item)
                    nc.scalar.copy(xnT_next[:], misc[:]).then_inc(s_next, 1)
                    act.wait_ge(s_next, 1 if b is None else b + 2)
                    act.sem_inc(s_free, 1)
                elif kind == "logits":
                    act.wait_ge(s_lshift, 1 if b is None else b + 2)
                    nc.scalar.activation(lexp[:], lshift[:], ACT.Exp).then_inc(s_lexp, 1)
                elif kind == "latent":
                    filled(b, prep, item)
                    nc.scalar.copy(latT[:], misc[:]).then_inc(s_lat, 1)
                    act.wait_ge(s_lat, b + 1)
                    act.sem_inc(s_free, 1)
                elif kind == "query":
                    filled(b, prep, item)
                    act.wait_ge(s_qst0, 16 * b)
                    nc.scalar.copy(qparts[:, 0, :], misc[:]).then_inc(s_q1, 1)
                elif kind == "kstack":
                    filled(b, prep, item)
                    nc.scalar.copy(kst[:], misc16[:, 0:T]).then_inc(s_kst, 1)
                    act.wait_ge(s_kst, b + 1)
                    act.sem_inc(s_free, 1)
                elif kind == "b":
                    _, g, i = item
                    h0, n, tiles = B_BANKS[i]
                    act.wait_ge(s_b, B_ALL * b + NB * g + i + 1)
                    if i == 0:
                        act.wait_ge(s_pv, GROUPS * b + max(g - 1, 0))
                    c = PCOL[tiles[0]]
                    w = sum(T - s * P for s in tiles)
                    nc.scalar.activation(probT[:, g % 2, h0:h0 + n, c:c + w],
                                         scores_out(item).rearrange("p (h c) -> p h c", h=n), ACT.Exp,
                                         scale=SCALE).then_inc(s_exp, 1)
                elif kind == "pv":
                    g = item[1]
                    act.wait_ge(s_pv, GROUPS * b + g + 1)
                    if g:
                        act.wait_ge(s_misc, misc_use(b, prep, ("heads", g - 1)) + 1)
                    nc.scalar.copy(hraw[:], pvb[:]).then_inc(s_hraw, 1)
                elif kind == "turn":
                    filled(b, prep, item)
                    nc.scalar.copy(yT[:], misc[:]).then_inc(s_yT, 1)
                    act.wait_ge(s_yT, b + 1)
                    act.sem_inc(s_free, 1)
                elif kind == "out":
                    act.wait_ge(s_down, UNITS * (b + 1))
                    nc.scalar.copy(accs[:], acc[:]).then_inc(s_accs, 1)

            def sequence(b, prep):
                steps = plan(prep)
                for step in range(STEPS):
                    f, k = divmod(step, 3)
                    for item in steps[step]:
                        do(b, prep, item)
                    if k == 0:
                        act.wait_ge(s_g, UNITS * b + f + 1)
                        act.wait_ge(s_gfree, UNITS * b + max(f - 1, 0))
                        nc.scalar.activation(th[:, f % 2, :], gb[:], ACT.Tanh, scale=0.5).then_inc(s_th, 1)
                for item in steps[STEPS]:
                    do(b, prep, item)

            for item in PREPARE:
                do(None, True, item)
            sequences(act, sequence, B)

        @block.vector
        def _(dve):
            count = {"local": 0, "before": 0, "per": 0}

            def link(b, ins):
                count["local"] += 1
                ins.then_inc(s_dve, 1)
                base = 0 if b is None else count["before"] + b * count["per"]
                dve.wait_ge(s_dve, base + count["local"])

            def filled(b, prep, item):
                dve.wait_ge(s_misc, misc_use(b, prep, item) + 1)

            def grid(ap, n=TB):
                return ap.rearrange("p (t e) -> p t e", t=n)

            def spread(ap, n):
                return ap.unsqueeze(2).broadcast_to([P, ap.shape[1], n])

            def apart():
                dve.sem_inc(s_apart, 1)

            def do(b, prep, item):
                kind = item[0]
                nxt = 1 if b is None else b + 2
                if kind == "norm":
                    dve.wait_ge(s_xt, 16 * nxt)
                    for t in range(TB):
                        last = nc.vector.bn_stats(stats[:, t, :], xt[:, t, :])
                    link(b, last)
                    apart()
                    for t in range(TB):
                        last = nc.vector.bn_aggr(meanvar[:, t, :], stats[:, t, :])
                    link(b, last)
                    nc.vector.tensor_scalar(vareps[:], meanvar[:, :, 1], EPS, None, ALU.add).then_inc(s_vareps, 1)
                    if b is not None:
                        dve.wait_ge(s_misc, MISC_BEFORE + b * MISC_PER)
                    dve.wait_ge(s_rstd, nxt)
                    for t in range(TB):
                        last = nc.vector.tensor_scalar(xn[:, t, :], xt[:, t, :], meanvar[:, t, 0:1], rstd[:, t:t + 1],
                                                       ALU.subtract, ALU.mult)
                    last.then_inc(s_norm, 1)
                elif kind == "logits":
                    filled(b, prep, item)
                    logits = grid(misc[:, 0:TB * EXPERTS])
                    link(b, nc.vector.tensor_reduce(lmax[:], logits, AX.X, ALU.max))
                    link(b, nc.vector.tensor_tensor(grid(lshift[:]), logits, spread(lmax[:], EXPERTS), ALU.subtract))
                    dve.sem_inc(s_free, 1)
                    dve.sem_inc(s_lshift, 1)
                elif kind == "route":
                    dve.wait_ge(s_lexp, nxt)
                    link(b, nc.vector.tensor_reduce(lsum[:], grid(lexp[:]), AX.X, ALU.add))
                    link(b, nc.vector.reciprocal(linv[:], lsum[:]))
                    link(b, nc.vector.tensor_tensor(grid(probs[:]), grid(lexp[:]), spread(linv[:], EXPERTS), ALU.mult))
                    apart()
                    for t in range(TB):
                        last = nc.vector.max(top[:, t, :], probs[:, t * EXPERTS:(t + 1) * EXPERTS])
                    link(b, last)
                    apart()
                    for t in range(TB):
                        last = nc.vector.max_index(topi[:, t, :], top[:, t, :], probs[:, t * EXPERTS:(t + 1) * EXPERTS])
                    link(b, last)
                    link(b, nc.vector.tensor_copy(topf[:], topi[:]))
                    numbers = number[:].unsqueeze(1).broadcast_to([P, TB, EXPERTS])
                    nc.vector.tensor_tensor(grid(first[:]), numbers, spread(topf[:, :, 0], EXPERTS), ALU.is_equal)
                    link(b, nc.vector.tensor_tensor(grid(second[:]), numbers, spread(topf[:, :, 1], EXPERTS), ALU.is_equal))
                    link(b, nc.vector.tensor_tensor(first[:], first[:], second[:], ALU.add))
                    link(b, nc.vector.scalar_tensor_tensor(out=gates[:], in0=first[:], scalar=ROUTED, in1=probs[:],
                                                           op0=ALU.mult, op1=ALU.mult))
                    link(b, nc.vector.tensor_copy(gparts[:, :, 0:8], grid(gates[:])))
                    link(b, nc.vector.tensor_tensor(grid(gleft[:]), grid(gates[:]), gparts[:, :, 0:8], ALU.subtract))
                    link(b, nc.vector.tensor_copy(gparts[:, :, 32:40], grid(gleft[:])))
                    nc.vector.tensor_tensor(gparts[:, :, 64:72], grid(gleft[:]), gparts[:, :, 32:40],
                                            ALU.subtract).then_inc(s_gparts, 1)
                elif kind == "gates":
                    filled(b, prep, item)
                    link(b, nc.vector.tensor_copy(gpartsT[:], misc16[0:96, 0:T]))
                    dve.sem_inc(s_free, 1)
                    dve.sem_inc(s_gT, 1)
                elif kind == "query":
                    dve.wait_ge(s_q1, b + 1)
                    link(b, nc.vector.tensor_tensor(qleft[:], misc[:], qparts[:, 0, :], ALU.subtract))
                    dve.sem_inc(s_free, 1)
                    link(b, nc.vector.tensor_copy(qparts[:, 1, :], qleft[:]))
                    nc.vector.tensor_tensor(qparts[:, 2, :], qleft[:], qparts[:, 1, :], ALU.subtract).then_inc(s_q, 1)
                elif kind == "keys":
                    filled(b, prep, item)
                    kv = grid(misc[:, 0:TB * 2 * HD])
                    nc.vector.tensor_copy(vaug[:, :, 0:HD], kv[:, :, HD:2 * HD])
                    link(b, nc.vector.tensor_copy(krows[:, :, 0:HD], kv[:, :, 0:HD]))
                    link(b, nc.vector.tensor_tensor(kleft[:], kv[:, :, 0:HD], krows[:, :, 0:HD], ALU.subtract))
                    dve.sem_inc(s_free, 1)
                    link(b, nc.vector.tensor_copy(krows[:, :, HD:2 * HD], kleft[:]))
                    link(b, nc.vector.tensor_tensor(krows[:, :, 2 * HD:3 * HD], kleft[:], krows[:, :, HD:2 * HD],
                                                    ALU.subtract))
                    nc.vector.tensor_copy(krows[:, :, 24:48], krows[:, :, 0:24])
                    nc.vector.tensor_copy(krows[:, :, 48:72], krows[:, :, 0:24]).then_inc(s_krows, 1)
                elif kind == "gate":
                    e = item[1]
                    filled(b, prep, item)
                    dve.wait_ge(s_u, UNITS * b + FC * (e - 1) if e > 1 else UNITS * b)
                    ins = nc.vector.tensor_tensor(xe[:, e % 2, :], misc[:], xnT[:], ALU.mult)
                    link(b, ins)
                    dve.sem_inc(s_free, 1)
                    dve.sem_inc(s_xe, 1)
                elif kind == "a":
                    _, g, i = item
                    t, h0, n = A_BANKS[i]
                    dve.wait_ge(s_a, A_ALL * b + NA * g + i + 1)
                    keys = (t + 1) * P
                    nc.vector.tensor_reduce(nmax[:, t, HG * g + h0:HG * g + h0 + n],
                                            scores_out(item)[:, 0:n * keys].rearrange("p (h s) -> p h s", h=n), AX.X,
                                            ALU.max, negate=True).then_inc(s_amax, 1)
                elif kind == "maxima":
                    g = item[1]
                    m = nmax[:, :, HG * g:HG * g + HG]
                    dve.wait_ge(s_amax, A_ALL * b + NA * (g + 1))
                    link(b, nc.vector.tensor_copy(mparts[:, :, 0, :], m))
                    link(b, nc.vector.tensor_tensor(mleft[:], m, mparts[:, :, 0, :], ALU.subtract))
                    link(b, nc.vector.tensor_copy(mparts[:, :, 1, :], mleft[:]))
                    nc.vector.tensor_tensor(mparts[:, :, 2, :], mleft[:], mparts[:, :, 1, :],
                                            ALU.subtract).then_inc(s_mparts, 1)
                    filled(b, prep, item)
                    dve.wait_ge(s_mst, 16 * (GROUPS * b + g))
                    link(b, nc.vector.tensor_copy(mT[:], misc16[0:PARTS * HG, 0:T]))
                    dve.sem_inc(s_free, 1)
                    dve.sem_inc(s_mT, 1)
                elif kind == "heads":
                    g = item[1]
                    filled(b, prep, item)
                    sums = misc[:].rearrange("p (n r) -> p n r", r=32)
                    link(b, nc.vector.reciprocal(dinv[:], sums[:, :, HD]))
                    link(b, nc.vector.tensor_tensor(y[:, :, 32 * g:32 * g + 32].rearrange("p t (h d) -> p t h d", d=HD),
                                                    sums[:, :, 0:HD].rearrange("p (t h) d -> p t h d", t=TB),
                                                    dinv[:].rearrange("p (t h) -> p t h", t=TB).unsqueeze(3).broadcast_to([P, TB, HG, HD]),
                                                    ALU.mult))
                    dve.sem_inc(s_free, 1)
                    dve.sem_inc(s_y, 1)
                elif kind == "out":
                    filled(b, prep, item)
                    dve.wait_ge(s_xres, 16 * (b + 1))
                    dve.wait_ge(s_out, 16 * b)
                    link(b, nc.vector.tensor_tensor(res[:].rearrange("p t d -> p (t d)"), misc[:],
                                                    xres[:].rearrange("p t d -> p (t d)"), ALU.add))
                    dve.sem_inc(s_free, 1)
                    dve.sem_inc(s_res, 1)

            def sequence(b, prep):
                steps = plan(prep)
                count["local"] = 0
                dve.wait_ge(s_down, UNITS * b)
                nc.vector.tensor_copy(xnT[:], xnT_next[:]).then_inc(s_xnT, 1)
                nc.vector.tensor_scalar(xe[:, 0, :], xnT_next[:], SHARED, None, ALU.mult).then_inc(s_xe, 1)
                for step in range(STEPS):
                    f, k = divmod(step, 3)
                    for item in steps[step]:
                        do(b, prep, item)
                    if k == 1:
                        dve.wait_ge(s_h, UNITS * b + f)
                        dve.wait_ge(s_th, UNITS * b + f + 1)
                        nc.vector.scalar_tensor_tensor(out=ga[:], in0=th[:, f % 2, :], scalar=1.0, in1=gb[:],
                                                       op0=ALU.add, op1=ALU.mult).then_inc(s_gfree, 1)
                    elif k == 2:
                        dve.wait_ge(s_u, UNITS * b + f + 1)
                        dve.wait_ge(s_gfree, UNITS * b + f + 1)
                        dve.wait_ge(s_down, UNITS * b + max(f - 1, 0))
                        nc.vector.tensor_tensor(hid[:, f % 2, :], ga[:], ub[:], ALU.mult).then_inc(s_h, 1)
                for item in steps[STEPS]:
                    do(b, prep, item)
                return count["local"]

            dve.wait_ge(s_gwT, 1)
            nc.vector.tensor_copy(gwT[:], acc[:, 0:EXPERTS]).then_inc(s_gwTs, 1)
            dve.wait_ge(s_const, 1)
            nc.vector.tensor_copy(number[:], number_i[:])
            for item in PREPARE:
                do(None, True, item)
            count["before"] = count["local"]
            dve.wait_ge(s_next, 1)
            each = {"norm": 2, "logits": 2, "route": 12, "gates": 1, "query": 2, "keys": 4, "gate": 1, "maxima": 4,
                    "heads": 2, "out": 1}
            count["per"] = sum(each.get(i[0], 0) for i in flat[True])

            def checked(b, prep):
                n = sequence(b, prep)
                assert n == sum(each.get(i[0], 0) for i in flat[prep]), (n, count)

            sequences(dve, checked, B)

        @block.gpsimd
        def _(pool):
            for t in (wdown, wq, wkv):
                last = nc.gpsimd.memset(t[:], 0.0)
            last.then_inc(s_zero, 1)
            nc.gpsimd.memset(ident[:], 0.0)
            nc.gpsimd.memset(never[:], 0.0)
            nc.gpsimd.memset(pick[:], 0.0)
            nc.gpsimd.memset(gparts[:], 0.0)
            nc.gpsimd.memset(krows[:], 0.0)
            nc.gpsimd.memset(vaug[:], 0.0)
            nc.gpsimd.memset(minus_half[:], -0.5)
            nc.gpsimd.iota(number_i[:], pattern=[[1, EXPERTS]], base=0, channel_multiplier=0)
            nc.gpsimd.memset(qst[:].rearrange("p h t -> p (h t)").bitcast(F32), 0.0).then_inc(s_zero, 1)
            pool.wait_ge(s_zero, 2)
            nc.gpsimd.affine_select(out=ident[:], in_=ident[:], compare_op=ALU.not_equal, fill=1.0, base=0,
                                    pattern=[[-1, P]], channel_multiplier=1)
            nc.gpsimd.affine_select(out=never[:], in_=never[:], compare_op=ALU.is_ge, fill=NEVER, base=0,
                                    pattern=[[-1, P]], channel_multiplier=1)
            for i in range(PARTS):
                nc.gpsimd.affine_select(out=pick[:], in_=pick[:], compare_op=ALU.not_equal, fill=1.0, base=-32 * i,
                                        pattern=[[-1, EXPERTS], [0, P]], channel_multiplier=1).then_inc(s_zero, 1)
                pool.wait_ge(s_zero, 3 + i)
            nc.gpsimd.memset(krows[:, :, MROW:STACKED], 1.0)
            nc.gpsimd.memset(vaug[:, :, HD:HD + 1], 1.0).then_inc(s_zero, 1)
            pool.wait_ge(s_zero, 3 + PARTS)
            nc.gpsimd.tensor_copy(ident16[:], ident[:]).then_inc(s_const, 1)

            def do(b, item):
                kind = item[0]
                nxt = 1 if b is None else b + 2
                if kind == "norm":
                    pool.wait_ge(s_vareps, nxt)
                    nc.gpsimd.tensor_tensor(rstd[:], vareps[:], minus_half[:], ALU.pow).then_inc(s_rstd, 1)

            def sequence(b, prep):
                for step in plan(prep):
                    for item in step:
                        do(b, item)

            do(None, ("norm",))
            sequences(pool, sequence, B)


_INS = ["L0_attn_x", "L0_attn_Wc_down", "L0_attn_Wq_up", "L0_attn_Wkv_up", "L0_attn_Wc_proj", "L0_ffn_gate_W",
        "L0_ffn_w1_e", "L0_ffn_w3_e", "L0_ffn_w2_e", "L0_ffn_w1_s", "L0_ffn_w3_s", "L0_ffn_w2_s"]


def kernel(**inputs):
    import numpy as _np
    import concourse.bacc as _bacc
    from concourse.bass_utils import run_bass_kernel_spmd as _run

    nc = _bacc.Bacc("TRN2", target_bir_lowering=False, num_devices=1)
    arrays, args = {}, []
    for name in _INS:
        a = _np.ascontiguousarray(inputs[name])
        arrays[f"in_{name}"] = a
        args.append(nc.dram_tensor(f"in_{name}", a.shape, mybir.dt.from_np(a.dtype), kind="ExternalInput").ap())
    shape = arrays["in_L0_attn_x"].shape
    args.append(nc.dram_tensor("out_0", shape, F32, kind="ExternalOutput").ap())
    build(nc, *args)
    r = _run(nc, [arrays], core_ids=[0])
    return r.results[0]["out_0"]
```

```python
from contextlib import ExitStack

import concourse.bass as bass
from concourse import mybir

F32 = mybir.dt.float32
BF16 = mybir.dt.bfloat16
U32 = mybir.dt.uint32
I32 = mybir.dt.int32
ALU = mybir.AluOpType
ACT = mybir.ActivationFunctionType
AX = mybir.AxisListType

P = 128
D = 128
LAT = 64
HEADS, HD = 16, 8
GROUPS = 4
HG = HEADS // GROUPS
TB = 4
T = TB * P
B = 8
NT = B * TB
N = NT * P
EXPERTS, TOPK = 8, 2
F = 512
FC = F // P
EPS = 1e-5
SCALE = HD ** -0.5
NEVER = -3.0e38
ROUTED = 0.5 * 0.5
SHARED = 0.5 * 0.5 / 8

TILES = N * TOPK // P + EXPERTS
MIDDLE = B - 2
PER = 11
REST = TILES - PER * MIDDLE
assert 0 < REST <= PER
PAD = N

PARTS = 3
MROW = 96
STACKED = MROW + PARTS
PAYLOAD = 3 + PARTS

PCOL = {0: 0, 1: 512, 3: 896, 2: 1024}
PCOLS = 1280

A_BANKS = [(3, 0, 1), (3, 1, 1), (3, 2, 1), (3, 3, 1), (2, 0, 1), (2, 1, 1), (2, 2, 1), (2, 3, 1),
           (1, 0, 2), (1, 2, 2), (0, 0, 4)]
B_BANKS = [(h, 1, (0,)) for h in range(HG)] + [(h, 1, (1, 3)) for h in range(HG)] + [(0, 2, (2,)), (2, 2, (2,))]
NA, NB = len(A_BANKS), len(B_BANKS)
RING = 4
DEEP = 3
A_ALL, B_ALL = GROUPS * NA, GROUPS * NB

FIRST, MID, LAST = "first", "middle", "last"
SHARE = {FIRST: 0, MID: PER, LAST: REST}
UNITS = {kind: FC + SHARE[kind] for kind in SHARE}


PACE = {FIRST: dict(first=14, group=13, turn=14.5, b=20.5, pv=35, heads=37.5, early=3, end=90),
        MID: dict(first=11, group=12, turn=13.5, b=19.5, pv=33.5, heads=36, early=4, end=94),
        LAST: dict(first=11, group=11, turn=12.5, b=18.5, pv=31, heads=33.5, early=4, end=66)}


def plan(kind):
    pace = PACE[kind]
    at = []

    def put(time, *item):
        at.append((time, len(at), item))

    put(0.5, "latent")
    put(1.7, "query")
    put(3, "keys")
    put(6, "kstack")
    for g in range(GROUPS):
        start = pace["first"] + pace["group"] * g
        for i in range(NA):
            put(start + pace["group"] * i / NA, "a", g, i)
        put(start + pace["group"] * (NA - 0.9) / NA, "split", g)
        put(start + pace["turn"], "maxima", g)
        for i in range(NB):
            put(start + pace["b"] + pace["group"] * i / NB, "b", g, i)
        put(start + pace["pv"], "pv", g)
        put(start + pace["heads"], "heads", g)
    last = pace["first"] + pace["group"] * (GROUPS - 1) + pace["heads"]
    put(last + 2, "turn")
    put(last + 4, "project")
    put(last + 6.5, "out")
    units, early = UNITS[kind], pace["early"]

    def due(n):
        return (pace["first"] * n / early if n <= early else
                pace["first"] + (pace["end"] - pace["first"]) * (n - early) / (units - early))

    for n in range(units):
        span = due(n + 1) - due(n)
        put(due(n), "g", n)
        if n + 1 >= FC and n + 1 < units:
            put(due(n) + 0.25 * span, "xs", n + 1)
        put(due(n) + 0.5 * span, "u", n)
        if n:
            put(due(n) + 0.75 * span, "fin", n - 1)
        put(due(n) + 0.8 * span, "mul", n)
    put(due(units) - 0.6, "fin", units - 1)
    if kind == FIRST:
        put(0, "choose")
        put(8, "prefix")
        put(8.1, "place")
        for i in range(NT):
            put(12 + 2.2 * i, "hot", i)
            put(12 + 2.2 * (i + 1.5), "slot", i)
        put(88, "table")
    else:
        put(5, "ids")
    if kind == LAST:
        for c in range(B):
            put(pace["end"] + 3 + c, "merge", c)
    return [item for _, _, item in sorted(at)]


def in_turn(item):
    return item[0] in ("latent", "query", "keys", "kstack", "maxima", "heads", "turn", "out")


def in_ring(item):
    return item[0] in ("a", "b", "pv") or in_turn(item)


def places(items, wanted):
    return {item: n for n, item in enumerate(i for i in items if wanted(i))}


def before(b, first, each):
    return 0 if isinstance(b, int) and b == 0 else each * b + (first - each)


def sequences(eng, run):
    run(0, FIRST)
    with eng.Fori(1, B - 1) as b:
        run(b, MID)
    run(B - 1, LAST)


def build(nc, x, Wc_down, Wq_up, Wkv_up, Wc_proj, gate_W, w1_e, w3_e, w2_e, w1_s, w3_s, w2_s, out):
    items = {kind: plan(kind) for kind in (FIRST, MID, LAST)}
    turn_at = {kind: places(items[kind], in_turn) for kind in items}
    TURNS = len(turn_at[MID])
    ring_items = {kind: [i for i in items[kind] if in_ring(i)] for kind in items}
    ring_at = {kind: places(items[kind], in_ring) for kind in items}
    assert ring_items[FIRST][-RING:] == ring_items[MID][-RING:]

    with ExitStack() as ctx:
        def sb(name, shape, dt=F32):
            return ctx.enter_context(nc.sbuf_tensor(name, shape, dt))

        def bank(name, shape):
            return ctx.enter_context(nc.psum_tensor(name, shape, F32))

        def sem(name):
            return ctx.enter_context(nc.semaphore(name))

        ring = bank("ring", [P, RING, 512])
        gb = bank("gb", [P, 512])
        ub = bank("ub", [P, 512])
        acc = bank("acc", [P, 512])
        slotb = bank("slotb", [P, 512])

        w13 = sb("w13", [P, 1 + EXPERTS, 2, F])
        w1, w3 = w13[:, :, 0, :], w13[:, :, 1, :]
        w2 = sb("w2", [P, 1 + EXPERTS, FC, D])
        w13_now = sb("w13_now", [P, 2, 2, F])
        w2_now = sb("w2_now", [P, 2, FC, D])
        wdown = sb("wdown", [P, P])
        wq = sb("wq", [P, P])
        wkv = sb("wkv", [P, 2 * HD])
        wproj = sb("wproj", [P, D])
        gw = sb("gw", [EXPERTS, D])
        gwT = sb("gwT", [P, EXPERTS])
        ident = sb("ident", [P, P])
        ident16 = sb("ident16", [P, P], BF16)
        never = sb("never", [P, P], BF16)
        earlier = sb("earlier", [P, P], BF16)
        ones16 = sb("ones16", [P, P], BF16)
        count_i = sb("count_i", [P, P], I32)
        count_f = sb("count_f", [P, P])
        lane_i = sb("lane_i", [P, 1], I32)
        lane = sb("lane", [P, 1])
        pad_row = sb("pad_row", [P, 1])
        pad_minus = sb("pad_minus", [P, 1])
        minus_half = sb("minus_half", [P, NT])
        zeros = sb("zeros", [P, P])
        x_all = sb("x_all", [P, NT, D])
        xnT = sb("xnT", [P, N])
        stats = sb("stats", [P, NT, 6])
        meanvar = sb("meanvar", [P, NT, 2])
        vareps = sb("vareps", [P, NT])
        rstd = sb("rstd", [P, NT])
        lmax = sb("lmax", [P, NT])
        linv = sb("linv", [P, NT])
        best = sb("best", [P, TOPK, NT])
        rank1 = sb("rank1", [P, NT])
        tiles_of = sb("tiles_of", [P, EXPERTS])
        tile_end = sb("tile_end", [P, EXPERTS])
        tile_begin = sb("tile_begin", [P, EXPERTS])
        slot_f = sb("slot_f", [P, TOPK, NT])
        slot_i = sb("slot_i", [P, TOPK, NT], I32)
        row_i = sb("row_i", [P, TOPK, NT], I32)
        col_f = sb("col_f", [P, TOPK, NT])
        row_f = sb("row_f", [P, TOPK, NT])
        gate_f = sb("gate_f", [P, TOPK, NT])
        payload = sb("payload", [P, TOPK, NT, PAYLOAD], BF16)
        row_hot = sb("row_hot", [P, DEEP, TOPK, P], BF16)
        col_hot = sb("col_hot", [P, DEEP, TOPK, TILES], BF16)
        loaded = sb("loaded", [P, DEEP, TOPK, PAYLOAD, TILES], BF16)
        ids = sb("ids", [P, TILES], U32)
        gates = sb("gates", [P, TILES])
        experts_f = sb("experts_f", [1, TILES])
        experts = sb("experts", [1, TILES], I32)
        ids_now = sb("ids_now", [P, PER], U32)
        gates_now = sb("gates_now", [P, PER])
        latT = sb("latT", [P, T])
        qparts = sb("qparts", [P, PARTS, T], BF16)
        qleft = sb("qleft", [P, T])
        qst = sb("qst", [P, HEADS, T], BF16)
        kleft = sb("kleft", [P, TB, HD])
        krows = sb("krows", [P, TB, P], BF16)
        kst = sb("kst", [P, T], BF16)
        vaug = sb("vaug", [P, TB, 32])
        nmax = sb("nmax", [P, TB, HEADS])
        mleft = sb("mleft", [P, TB, HG])
        mparts = sb("mparts", [P, TB, PARTS, HG], BF16)
        mT = sb("mT", [PARTS * HG, T], BF16)
        probT = sb("probT", [P, 2, HG, PCOLS])
        hraw = sb("hraw", [P, T])
        dinv = sb("dinv", [P, TB * HG])
        y = sb("y", [P, TB, D])
        yT = sb("yT", [P, T])
        xs = sb("xs", [P, 3, D])
        xsT = sb("xsT", [P, 2, P])
        th = sb("th", [P, 2, F])
        ga = sb("ga", [P, F])
        hid = sb("hid", [P, 2, F])
        ys = sb("ys", [P, 3, D])
        accs = sb("accs", [P, T])
        found_room = sb("found", [P, PAYLOAD * TILES])
        rbuf = loaded[:].rearrange("p i k c n -> p (i k c n)").bitcast(F32)[:, 0:2 * TB * D].rearrange("p (k f) -> p k f", k=2)

        spare = probT[:].rearrange("p a h c -> p (a h c)")
        xn = spare[:, 0:N].rearrange("p (t d) -> p t d", d=D)
        NE = NT * EXPERTS
        room = [spare[:, N + NE * i:N + NE * (i + 1)] for i in range(14)]
        (lshift, lexp, probs, same, first, probs2, second, weight, cumul, rank, thresh, restart, picked,
         mask_room) = room
        mask16 = mask_room.bitcast(BF16)[:, 0:NE]
        grid = spare[0:1, N + 14 * NE:N + 14 * NE + TILES * EXPERTS]
        assert N + 14 * NE + TILES * EXPERTS <= 2 * HG * PCOLS

        q_dram = nc.dram_tensor("q_scratch", (PARTS, HEADS, HD, T), BF16, kind="Internal").ap()
        m_dram = nc.dram_tensor("m_scratch", (GROUPS, PARTS, HG, T), BF16, kind="Internal").ap()
        xn_dram = nc.dram_tensor("xn_scratch", (N + P, D), F32, kind="Internal").ap()
        r_dram = nc.dram_tensor("routed_scratch", (N + P, D), F32, kind="Internal").ap()

        s_w = [sem(f"weights_loaded_{e}") for e in range(1 + EXPERTS)]
        s_small = sem("small_weights_loaded")
        s_zero = sem("buffers_zeroed")
        s_const = sem("constants_made")
        s_gwT = sem("gate_weights_turned")
        s_gwTs = sem("gate_weights_saved")
        s_xl = [sem(f"x_loaded_{c}") for c in range(B)]
        s_vareps = sem("variance_ready")
        s_rstd = sem("rstd_ready")
        s_norm = sem("normed")
        s_xnst = sem("xn_stored")
        s_turn = sem("x_turned")
        s_xnT = sem("xnT_ready")
        s_logits = sem("logits_ready")
        s_lread = sem("logits_read")
        s_lexp = sem("logits_exped")
        s_mask = sem("choices_ready")
        s_prefix = sem("ranks_counted")
        s_spare = sem("routing_done_with_room")
        s_place = sem("places_ready")
        s_hot = sem("one_hot_tiles_ready")
        s_made0 = sem("constants_begun")
        s_ident = sem("identity_made")
        s_made = sem("slot_operands_made_vector")
        s_madep = sem("slot_operands_made_pool")
        s_slot = sem("slots_added")
        s_table = sem("table_ready")
        s_ids = sem("ids_ready")
        s_lat = sem("latent_ready")
        s_q1 = sem("query_first_part")
        s_qread = sem("query_read")
        s_q = sem("query_parts_ready")
        s_qst0 = sem("query_parts_stored")
        s_qst = sem("query_stack_loaded")
        s_krows = sem("key_rows_ready")
        s_kread = sem("keys_read")
        s_kst = sem("key_stack_ready")
        s_a = sem("a_scored")
        s_amax = sem("a_maxed")
        s_mparts = sem("maxima_parts_ready")
        s_mT = sem("maxima_turned")
        s_mst = sem("maxima_stored")
        s_m = [sem(f"maxima_loaded_{g}") for g in range(GROUPS)]
        s_b = sem("b_scored")
        s_exp = sem("b_exped")
        s_pv = sem("heads_summed")
        s_hraw = sem("heads_saved")
        s_y = sem("heads_normed")
        s_yT = sem("yT_ready")
        s_misc = sem("turned_or_product_in_ring")
        s_xs = [sem(f"slot_rows_gathered_{k}") for k in range(3)]
        s_xt = sem("slot_rows_turning")
        s_xsT = sem("slot_rows_turned")
        s_g = sem("g_ready")
        s_th = sem("tanh_done")
        s_gfree = sem("g_read")
        s_u = sem("u_ready")
        s_h = sem("hidden_ready")
        s_fin = sem("units_finished")
        s_w13 = [sem(f"expert_in_weights_staged_{k}") for k in range(2)]
        s_w2 = [sem(f"expert_out_weights_staged_{k}") for k in range(2)]
        s_ys = sem("slot_result_ready")
        s_scat = sem("routed_rows_added")
        s_accfull = sem("acc_ready")
        s_accs = sem("acc_saved")
        s_res = sem("result_ready")
        s_rl = [sem(f"routed_rows_loaded_{k}") for k in range(2)]
        s_merged = sem("merged")
        s_out = sem("result_stored")
        s_dve = sem("vector_step")
        s_apart = sem("waits_carried")

        def turns(b, kind, item):
            return TURNS * b + turn_at[kind][item] + 1

        def units(b):
            return before(b, UNITS[FIRST], UNITS[MID])

        def tiles(b):
            return PER * b - PER

        def staged(b, j):
            return 16 * (((PER + 1 - j % 2) // 2) * (b - 1) + j // 2 + 1)

        def gathered(b, j):
            return 16 * (((PER + 2 - j % 3) // 3) * (b - 1) + j // 3 + 1)

        def bank_of(kind, item):
            return ring[:, ring_at[kind][item] % RING, :]

        def bank16(kind, item):
            return bank_of(kind, item).bitcast(BF16)

        def read(b, item):
            what, g = item[0], item[1] if len(item) > 1 else 0
            return {"latent": (s_lat, b + 1), "query": (s_qread, b + 1), "keys": (s_kread, b + 1),
                    "kstack": (s_kst, b + 1), "maxima": (s_mT, GROUPS * b + g + 1), "heads": (s_y, GROUPS * b + g + 1),
                    "turn": (s_yT, b + 1), "out": (s_res, b + 1), "pv": (s_hraw, GROUPS * b + g + 1),
                    "a": (s_amax, A_ALL * b + NA * g + item[-1] + 1 if what == "a" else 0),
                    "b": (s_exp, B_ALL * b + NB * g + item[-1] + 1 if what == "b" else 0)}[what]

        block = ctx.enter_context(nc.Block())

        @block.sync
        def _(sp):
            x_tiles = x.rearrange("b (t p) d -> b p t d", p=P)
            out_tiles = out.rearrange("b (t p) d -> b p t d", p=P)
            for c in range(B):
                sp.dma_start(x_all[:, TB * c:TB * c + TB, :], x_tiles[c]).then_inc(s_xl[c], 16)
            sp.dma_start(gw[:], gate_W).then_inc(s_small, 16)
            sp.wait_ge(s_zero, 1)
            sp.dma_start(wdown[:, 0:LAT], Wc_down).then_inc(s_small, 16)
            sp.dma_start(wq[0:LAT, :], Wq_up).then_inc(s_small, 16)
            sp.dma_start(wkv[0:LAT, :], Wkv_up).then_inc(s_small, 16)
            sp.dma_start(wproj[:], Wc_proj).then_inc(s_small, 16)
            for c in range(B):
                sp.wait_ge(s_norm, c + 1)
                rows = xn_dram[c * T:(c + 1) * T, :].rearrange("(t p) d -> p t d", p=P)
                sp.dma_start(rows, xn[:, TB * c:TB * c + TB, :]).then_inc(s_xnst, 16)
            sp.dma_start(xn_dram[N:N + P, :], zeros[:]).then_inc(s_xnst, 16)
            for e in range(EXPERTS):
                sp.dma_start(w1[:, 1 + e, :], w1_e[e]).then_inc(s_w[1 + e], 16)
                sp.dma_start(w3[:, 1 + e, :], w3_e[e]).then_inc(s_w[1 + e], 16)
                sp.dma_start(w2[:, 1 + e, :, :], w2_e[e].rearrange("(c p) d -> p c d", p=P)).then_inc(s_w[1 + e], 16)

            def wait(s, n):
                sp.wait_ge(s, n)
                sp.sem_inc(s_apart, 1)

            def stage_in(b, j):
                wait(s_u, units(b) + (FC + j - 1 if j >= 2 else 0))
                e = sp.value_load(experts[0:1, bass.ds(tiles(b) + j, 1)], min_val=0, max_val=EXPERTS - 1)
                sp.dma_start(w13_now[:, j % 2], w13[:, e + 1]).then_inc(s_w13[j % 2], 16)
                return e

            def stage_out(b, j, e):
                wait(s_fin, units(b) + (FC + j - 1 if j >= 2 else 0))
                sp.dma_start(w2_now[:, j % 2], w2[:, e + 1]).then_inc(s_w2[j % 2], 16)

            def do(b, kind, item):
                what = item[0]
                if what == "latent" and kind != FIRST:
                    for j in range(2):
                        expert[j] = stage_in(b, j)
                elif what == "query":
                    wait(s_q, b + 1)
                    sp.dma_start(q_dram.rearrange("i h d t -> (h d) i t"), qparts[:]).then_inc(s_qst0, 16)
                    wait(s_qst0, 16 * (b + 1))
                    if kind != FIRST:
                        wait(s_b, B_ALL * b)
                    else:
                        wait(s_zero, 2)
                    for i in range(PARTS):
                        for j in range(PARTS):
                            row = (i * PARTS + j) * HD
                            sp.dma_start(qst[row:row + HD, :, :], q_dram[i].rearrange("h d t -> d h t")).then_inc(s_qst, 16)
                    if kind != FIRST:
                        for j in range(2):
                            stage_out(b, j, expert[j])
                elif what == "u" and item[1] >= FC:
                    j = item[1] - FC
                    if j + 2 < SHARE[kind]:
                        expert[j % 2] = stage_in(b, j + 2)
                elif what == "fin" and item[1] >= FC:
                    j = item[1] - FC
                    if j + 2 < SHARE[kind]:
                        stage_out(b, j + 2, expert[j % 2])
                elif what == "maxima":
                    g = item[1]
                    wait(s_mT, GROUPS * b + g + 1)
                    sp.dma_start(m_dram[g].rearrange("i h t -> (i h) t"), mT[:]).then_inc(s_mst, 16)
                    wait(s_mst, 16 * (GROUPS * b + g + 1))
                    sp.dma_start(qst[MROW:STACKED, HG * g:HG * g + HG, :], m_dram[g]).then_inc(s_m[g], 16)

            expert = [None, None]

            def sequence(b, kind):
                for item in items[kind]:
                    do(b, kind, item)
                if kind == FIRST:
                    for e in range(1, 1 + EXPERTS):
                        sp.wait_ge(s_w[e], 48)
                    sp.wait_ge(s_table, 1)
                if kind == LAST:
                    sp.wait_ge(s_scat, 16 * (1 + TILES))
                    for c in range(B + 2):
                        if c < B:
                            if c >= 2:
                                sp.wait_ge(s_merged, c - 1)
                            rows = r_dram[c * T:(c + 1) * T, :].rearrange("(t p) d -> p t d", p=P)
                            sp.dma_start(rbuf[:, c % 2, :].rearrange("p (t d) -> p t d", d=D), rows).then_inc(s_rl[c % 2], 16)
                        if 2 <= c < B + 1:
                            sp.wait_ge(s_merged, c - 1)
                            sp.dma_start(out_tiles[c - 2], x_all[:, TB * (c - 2):TB * (c - 1), :]).then_inc(s_out, 16)
                    sp.wait_ge(s_res, B)
                    sp.dma_start(out_tiles[B - 1], x_all[:, TB * (B - 1):TB * B, :]).then_inc(s_out, 16)

            sequences(sp, sequence)
            sp.wait_ge(s_out, 16 * B)

        @block.tensor
        def _(pe):
            def transposes(of, eye, where, done):
                for t in range(TB):
                    last = nc.tensor.transpose(where(t), of(t), eye)
                last.then_inc(done, 1)

            def do(b, kind, item):
                what = item[0]
                if in_ring(item):
                    k = ring_at[kind][item]
                    o = bank_of(kind, item)
                    if k >= RING:
                        pe.wait_ge(*read(b, ring_items[kind][k - RING]))
                    elif kind != FIRST:
                        past = [n for n in range(len(ring_items[MID])) if n % RING == k][-1]
                        pe.wait_ge(*read(b - 1, ring_items[MID][past]))
                if what == "latent":
                    nc.tensor.matmul(o, wdown[:], xnT[:, bass.ds(b * T, T)], start=True, stop=True).then_inc(s_misc, 1)
                elif what == "query":
                    pe.wait_ge(s_lat, b + 1)
                    nc.tensor.matmul(o, wq[:], latT[:], start=True, stop=True).then_inc(s_misc, 1)
                elif what == "keys":
                    for t in range(TB):
                        last = nc.tensor.matmul(o[:, t * 2 * HD:(t + 1) * 2 * HD], latT[:, t * P:(t + 1) * P],
                                                wkv[:], start=(t == 0), stop=True, skip_group_check=True)
                    last.then_inc(s_misc, 1)
                elif what == "kstack":
                    pe.wait_ge(s_krows, b + 1)
                    transposes(lambda t: krows[:, t, :], ident16[:], lambda t: bank16(kind, item)[:, t * P:(t + 1) * P], s_misc)
                elif what in ("a", "b"):
                    if what == "a":
                        scores_a(b, kind, item)
                    else:
                        scores_b(b, kind, item)
                elif what == "maxima":
                    pe.wait_ge(s_mparts, GROUPS * b + item[1] + 1)
                    transposes(lambda t: mparts[:, t].rearrange("p i h -> p (i h)"), ident16[:],
                               lambda t: bank16(kind, item)[0:PARTS * HG, t * P:(t + 1) * P], s_misc)
                elif what == "pv":
                    pv(b, item[1], o)
                elif what == "heads":
                    pe.wait_ge(s_hraw, GROUPS * b + item[1] + 1)
                    transposes(lambda t: hraw[:, t * P:(t + 1) * P], ident[:], lambda t: o[:, t * P:(t + 1) * P], s_misc)
                elif what == "turn":
                    pe.wait_ge(s_y, GROUPS * (b + 1))
                    transposes(lambda t: y[:, t, :], ident[:], lambda t: o[:, t * P:(t + 1) * P], s_misc)
                elif what == "project":
                    pe.wait_ge(s_yT, b + 1)
                    nc.tensor.matmul(acc[:], wproj[:], yT[:], start=False, stop=True, skip_group_check=True).then_inc(s_accfull, 1)
                elif what == "out":
                    pe.wait_ge(s_accs, b + 1)
                    transposes(lambda t: accs[:, t * P:(t + 1) * P], ident[:], lambda t: o[:, t * P:(t + 1) * P], s_misc)
                elif what == "g":
                    n = item[1]
                    pe_wait(s_gfree, units(b) + n)
                    if n < FC:
                        nc.tensor.matmul(gb[:], w1[:, 0, n * P:(n + 1) * P], xnT[:, bass.ds(b * T, T)], start=True,
                                         stop=True).then_inc(s_g, 1)
                    else:
                        j = n - FC
                        pe.wait_ge(s_xsT, tiles(b) + j + 1)
                        pe.wait_ge(s_w13[j % 2], staged(b, j))
                        expert_product(gb, 0, j, s_g)
                elif what == "u":
                    n = item[1]
                    pe_wait(s_h, units(b) + n)
                    if n < FC:
                        nc.tensor.matmul(ub[:], w3[:, 0, n * P:(n + 1) * P], xnT[:, bass.ds(b * T, T)], start=True,
                                         stop=True).then_inc(s_u, 1)
                    else:
                        j = n - FC
                        expert_product(ub, 1, j, s_u)
                elif what == "xs":
                    j = item[1] - FC
                    pe.wait_ge(s_ys, tiles(b) + slot_uses(kind, item, "fin") + 1)
                    pe.wait_ge(s_xs[j % 3], gathered(b, j))
                    nc.tensor.transpose(slotb[:, 0:P], xs[:, j % 3, :], ident[:]).then_inc(s_xt, 1)
                elif what == "fin":
                    n = item[1]
                    pe.wait_ge(s_h, units(b) + n + 1)
                    if n < FC:
                        if n == 0:
                            if kind != FIRST:
                                pe.wait_ge(s_accs, b)
                        ins = nc.tensor.matmul(acc[:], w2[:, 0, n, :], hid[:, n % 2, :], start=(n == 0),
                                               stop=False, skip_group_check=True)
                        ins.then_inc(s_fin, 1)
                    else:
                        j = n - FC
                        pe.wait_ge(s_w2[j % 2], staged(b, j))
                        pe.wait_ge(s_xsT, tiles(b) + slot_uses(kind, item, "xs"))
                        if n < FC + 1 or slot_order(kind)[slot_order(kind).index(item) - 1][0] == "fin":
                            pe.wait_ge(s_ys, tiles(b) + j + 1)
                        for c in range(FC):
                            last = nc.tensor.matmul(slotb[:, 0:D], hid[:, n % 2, c * P:(c + 1) * P], w2_now[:, j % 2, c, :],
                                                    start=(c == 0), stop=(c == FC - 1))
                        last.then_inc(s_fin, 1)
                elif what == "prefix":
                    pe.wait_ge(s_mask, 1)
                    nc.tensor.matmul(slotb[:, 0:NE], earlier[:], mask16, start=True, stop=True, skip_group_check=True)
                    nc.tensor.matmul(slotb[:, NE:2 * NE], ones16[:], mask16, start=False, stop=True,
                                     skip_group_check=True).then_inc(s_prefix, 1)
                elif what == "slot":
                    i = item[1]
                    if i == 0:
                        pe.wait_ge(s_spare, 1)
                    pe.wait_ge(s_made, i + 1)
                    pe.wait_ge(s_madep, i + 1)
                    for k in range(TOPK):
                        ins = nc.tensor.matmul(slotb[:, 0:PAYLOAD * TILES], row_hot[:, i % DEEP, k, :],
                                               loaded[:, i % DEEP, k].rearrange("p c n -> p (c n)"),
                                               start=(i == 0 and k == 0), stop=(i == NT - 1 and k == TOPK - 1))
                    ins.then_inc(s_slot, 1)

            def expert_product(o, which, j, done):
                for c in range(FC):
                    last = nc.tensor.matmul(o[:, c * P:(c + 1) * P], w13_now[:, j % 2, which, c * P:(c + 1) * P],
                                            xsT[:, j % 2, :], start=(c == 0), stop=True, skip_group_check=True)
                last.then_inc(done, 1)

            def slot_order(kind):
                return [i for i in items[kind] if i[0] == "xs" or (i[0] == "fin" and i[1] >= FC)]

            def slot_uses(kind, item, what):
                order = slot_order(kind)
                return sum(i[0] == what for i in order[:order.index(item)])

            def pe_wait(s, n):
                if not (isinstance(n, int) and n == 0):
                    pe.wait_ge(s, n)

            def scores_a(b, kind, item):
                _, g, i = item
                t, h0, n = A_BANKS[i]
                if (g, i) == (0, 0):
                    pe.wait_ge(s_qst, 16 * PARTS * PARTS * (b + 1))
                    pe.wait_ge(s_kst, b + 1)
                keys = (t + 1) * P
                o = bank_of(kind, item)
                for h in range(n):
                    nc.tensor.matmul(o[:, h * keys:(h + 1) * keys], qst[0:MROW, HG * g + h0 + h, t * P:(t + 1) * P],
                                     kst[0:MROW, 0:keys], start=(h == 0), stop=False, skip_group_check=True)
                diagonal = o[:, 0:n * keys].rearrange("p (h s) -> p h s", h=n)[:, :, t * P:keys]
                nc.tensor.matmul(diagonal, ident16[:], never[:].unsqueeze(1).broadcast_to([P, n, P]), start=False,
                                 stop=True, skip_group_check=True).then_inc(s_a, 1)

            def scores_b(b, kind, item):
                _, g, i = item
                h0, n, key_tiles = B_BANKS[i]
                if i == 0:
                    pe.wait_ge(s_m[g], 16 * (b + 1))
                o = bank_of(kind, item)
                col = 0
                for h in range(h0, h0 + n):
                    for s in key_tiles:
                        w = T - s * P
                        nc.tensor.matmul(o[:, col:col + w], kst[0:STACKED, s * P:(s + 1) * P],
                                         qst[0:STACKED, HG * g + h, s * P:T], start=(col == 0), stop=False,
                                         skip_group_check=True)
                        col += w
                if len(key_tiles) * n == 1:
                    diagonal, eye = o[:, 0:P], ident16[:]
                else:
                    eye = ident16[:].unsqueeze(1).broadcast_to([P, 2, P])
                    diagonal = (o.rearrange("p (c w) -> p c w", w=P)[:, 0:4:3, :] if n == 1 else
                                o.rearrange("p (n c) -> p n c", n=2)[:, :, 0:P])
                nc.tensor.matmul(diagonal, never[:], eye, start=False, stop=True, skip_group_check=True).then_inc(s_b, 1)

            def pv(b, g, o):
                pe.wait_ge(s_exp, B_ALL * b + NB * (g + 1))
                for s in range(TB):
                    for h in range(HG):
                        c = PCOL[s]
                        last = nc.tensor.matmul(o[32 * h:32 * h + 32, s * P:T], vaug[:, s, :],
                                                probT[:, g % 2, h, c:c + T - s * P], start=(s == 0),
                                                stop=(s == TB - 1), skip_group_check=True)
                last.then_inc(s_pv, 1)

            pe.wait_ge(s_ident, 1)
            pe.wait_ge(s_small, 16 * 5)
            nc.tensor.transpose(acc[:, 0:EXPERTS], gw[:], ident[0:EXPERTS, 0:EXPERTS]).then_inc(s_gwT, 1)

            def logits(c):
                pe.wait_ge(s_xnT, c + 1)
                for t in range(TB * c, TB * c + TB):
                    last = nc.tensor.matmul(slotb[:, t * EXPERTS:(t + 1) * EXPERTS], xnT[:, t * P:(t + 1) * P], gwT[:],
                                            start=(t == 0), stop=True, skip_group_check=True)
                last.then_inc(s_logits, 1)

            for c in range(B):
                pe.wait_ge(s_norm, c + 1)
                if c >= 2:
                    pe.wait_ge(s_xnT, c - 1)
                transposes(lambda t: xn[:, TB * c + t, :], ident[:],
                           lambda t: (gb, ub)[c % 2][:, t * P:(t + 1) * P], s_turn)
                if c == 0:
                    pe.wait_ge(s_gwTs, 1)
                else:
                    logits(c - 1)
            logits(B - 1)

            def sequence(b, kind):
                if kind == FIRST:
                    pe.wait_ge(s_w[0], 48)
                    pe.wait_ge(s_const, 1)
                for item in items[kind]:
                    do(b, kind, item)

            sequences(pe, sequence)

        @block.scalar
        def _(act):
            act.dma_start(w1[:, 0, :].rearrange("p (n f) -> p n f", n=8), w1_s.rearrange("n d f -> d n f")).then_inc(s_w[0], 16)
            act.dma_start(w3[:, 0, :].rearrange("p (n f) -> p n f", n=8), w3_s.rearrange("n d f -> d n f")).then_inc(s_w[0], 16)
            act.dma_start(w2[:, 0, :, :], w2_s.rearrange("n f d -> (n f) d").rearrange("(c p) d -> p c d", p=P)).then_inc(s_w[0], 16)
            for c in range(B):
                act.wait_ge(s_turn, c + 1)
                nc.scalar.copy(xnT[:, c * T:(c + 1) * T], (gb, ub)[c % 2][:]).then_inc(s_xnT, 1)

            def filled(b, kind, item):
                act.wait_ge(s_misc, turns(b, kind, item))

            def do(b, kind, item):
                what = item[0]
                if what == "choose":
                    act.wait_ge(s_lread, 1)
                    nc.scalar.activation(lexp, lshift, ACT.Exp).then_inc(s_lexp, 1)
                elif what == "latent":
                    filled(b, kind, item)
                    nc.scalar.copy(latT[:], bank_of(kind, item)).then_inc(s_lat, 1)
                elif what == "query":
                    filled(b, kind, item)
                    if kind != FIRST:
                        act.wait_ge(s_qst0, 16 * b)
                    nc.scalar.copy(qparts[:, 0, :], bank_of(kind, item)).then_inc(s_q1, 1)
                elif what == "kstack":
                    filled(b, kind, item)
                    nc.scalar.copy(kst[:], bank16(kind, item)[:, 0:T]).then_inc(s_kst, 1)
                elif what == "b":
                    _, g, i = item
                    h0, n, key_tiles = B_BANKS[i]
                    act.wait_ge(s_b, B_ALL * b + NB * g + i + 1)
                    if i == 0:
                        if kind == FIRST and g == 0:
                            act.wait_ge(s_place, 1)
                            act.wait_ge(s_xnst, 16 * (B + 1))
                        if kind != FIRST or g >= 2:
                            act.wait_ge(s_pv, GROUPS * b + max(g - 1, 0))
                    c = PCOL[key_tiles[0]]
                    w = sum(T - s * P for s in key_tiles)
                    nc.scalar.activation(probT[:, g % 2, h0:h0 + n, c:c + w],
                                         bank_of(kind, item).rearrange("p (h c) -> p h c", h=n), ACT.Exp,
                                         scale=SCALE).then_inc(s_exp, 1)
                elif what == "pv":
                    g = item[1]
                    act.wait_ge(s_pv, GROUPS * b + g + 1)
                    if g:
                        act.wait_ge(s_misc, turns(b, kind, ("heads", g - 1)))
                    nc.scalar.copy(hraw[:], bank_of(kind, item)).then_inc(s_hraw, 1)
                elif what == "turn":
                    filled(b, kind, item)
                    nc.scalar.copy(yT[:], bank_of(kind, item)).then_inc(s_yT, 1)
                elif what == "out":
                    act.wait_ge(s_accfull, b + 1)
                    nc.scalar.copy(accs[:], acc[:]).then_inc(s_accs, 1)
                elif what == "g":
                    n = item[1]
                    act.wait_ge(s_g, units(b) + n + 1)
                    if kind != FIRST or n >= 2:
                        act.wait_ge(s_gfree, units(b) + max(n - 1, 0))
                    nc.scalar.activation(th[:, n % 2, :], gb[:], ACT.Tanh, scale=0.5).then_inc(s_th, 1)
                elif what == "xs":
                    j = item[1] - FC
                    act.wait_ge(s_xt, tiles(b) + j + 1)
                    act.wait_ge(s_u, units(b) + (item[1] - 1 if j >= 2 else 0))
                    nc.scalar.copy(xsT[:, j % 2, :], slotb[:, 0:P]).then_inc(s_xsT, 1)
                elif what == "fin" and item[1] >= FC:
                    j = item[1] - FC
                    act.wait_ge(s_fin, units(b) + item[1] + 1)
                    act.wait_ge(s_scat, 16 * (tiles(b) + 1 + max(j - 2, 0)))
                    nc.scalar.activation(ys[:, j % 3, :], slotb[:, 0:D], ACT.Copy, scale=gates_now[:, j:j + 1]).then_inc(s_ys, 1)

            def sequence(b, kind):
                for item in items[kind]:
                    do(b, kind, item)

            sequences(act, sequence)

        @block.vector
        def _(dve):
            count = {"local": 0, "base": 0}

            def link(ins):
                count["local"] += 1
                ins.then_inc(s_dve, 1)
                dve.wait_ge(s_dve, count["base"] + count["local"])

            def filled(b, kind, item):
                dve.wait_ge(s_misc, turns(b, kind, item))

            def by_token(ap):
                return ap.rearrange("p (t e) -> p t e", e=EXPERTS)

            def by_expert(ap):
                return ap.rearrange("p (e t) -> p e t", e=EXPERTS)

            def spread(ap, n):
                return ap.unsqueeze(2).broadcast_to([ap.shape[0], ap.shape[1], n])

            def tt(o, a, c, op):
                return nc.vector.tensor_tensor(o, a, c, op)

            def choose():
                dve.wait_ge(s_logits, B)
                logits = by_token(slotb[:, 0:NE])
                link(nc.vector.tensor_reduce(lmax[:], logits, AX.X, ALU.max))
                link(tt(by_token(lshift), logits, spread(lmax[:], EXPERTS), ALU.subtract))
                dve.sem_inc(s_lread, 1)
                link(nc.vector.tensor_scalar(by_token(weight), count_f[:, 0:EXPERTS].unsqueeze(1).broadcast_to([P, NT, EXPERTS]),
                                             -1.0, float(EXPERTS), ALU.mult, ALU.add))
                dve.wait_ge(s_lexp, 1)
                link(nc.vector.tensor_reduce(lmax[:], by_token(lexp), AX.X, ALU.add))
                link(nc.vector.reciprocal(linv[:], lmax[:]))
                link(tt(by_token(probs), by_token(lexp), spread(linv[:], EXPERTS), ALU.mult))
                for k, (of, chosen) in enumerate(((probs, first), (probs2, second))):
                    link(nc.vector.tensor_reduce(best[:, k, :], by_token(of), AX.X, ALU.max))
                    link(tt(by_token(same), by_token(of), spread(best[:, k, :], EXPERTS), ALU.is_equal))
                    link(tt(same, same, weight, ALU.mult))
                    link(nc.vector.tensor_reduce(rank1[:], by_token(same), AX.X, ALU.max))
                    link(tt(by_token(chosen), by_token(weight), spread(rank1[:], EXPERTS), ALU.is_equal))
                    if k == 0:
                        link(nc.vector.scalar_tensor_tensor(out=probs2, in0=first, scalar=-2.0, in1=probs, op0=ALU.mult,
                                                            op1=ALU.add))
                tt(by_expert(mask16).rearrange("p e t -> p t e"), by_token(first), by_token(second), ALU.add).then_inc(s_mask, 1)

            def place():
                numbers = count_f[:, 0:NT].unsqueeze(1).broadcast_to([P, EXPERTS, NT])
                link(nc.vector.tensor_scalar(by_expert(restart), numbers, 0.0, None, ALU.is_gt))
                link(nc.vector.tensor_scalar(by_expert(thresh), numbers, float(P), None, ALU.mult))
                dve.wait_ge(s_prefix, 1)
                within, total = slotb[:, 0:NE], slotb[:, NE:2 * NE]
                link(nc.vector.tensor_tensor_scan(out=cumul, data0=restart, data1=total, initial=0.0, op0=ALU.mult, op1=ALU.add))
                link(tt(rank, cumul, total, ALU.subtract))
                link(tt(rank, rank, within, ALU.add))
                dve.sem_inc(s_spare, 1)
                link(tt(by_expert(same), spread(by_expert(cumul)[:, :, NT - 1], NT), by_expert(thresh), ALU.is_gt))
                link(nc.vector.tensor_reduce(tiles_of[:], by_expert(same), AX.X, ALU.add))
                link(nc.vector.tensor_tensor_scan(out=tile_end[:], data0=restart[:, 1:1 + EXPERTS], data1=tiles_of[:],
                                                  initial=0.0, op0=ALU.mult, op1=ALU.add))
                link(tt(tile_begin[:], tile_end[:], tiles_of[:], ALU.subtract))
                link(nc.vector.scalar_tensor_tensor(out=by_expert(rank), in0=spread(tile_begin[:], NT), scalar=float(P),
                                                    in1=by_expert(rank), op0=ALU.mult, op1=ALU.add))
                for k, chosen in enumerate((first, second)):
                    link(tt(by_token(picked), by_token(chosen), by_expert(rank).rearrange("p e t -> p t e"), ALU.mult))
                    link(nc.vector.tensor_reduce(slot_f[:, k, :], by_token(picked), AX.X, ALU.add))
                link(nc.vector.tensor_copy(slot_i[:], slot_f[:]))
                link(nc.vector.tensor_scalar(row_i[:], slot_i[:], P - 1, None, ALU.bitwise_and))
                link(nc.vector.tensor_copy(row_f[:], row_i[:]))
                link(tt(col_f[:], slot_f[:], row_f[:], ALU.subtract))
                link(nc.vector.tensor_scalar(col_f[:], col_f[:], 1.0 / P, None, ALU.mult))
                flat = payload[:].rearrange("p k t c -> p (k t) c")
                link(nc.vector.tensor_scalar(gate_f[:], best[:], ROUTED, None, ALU.mult))
                nc.vector.tensor_scalar(flat[:, :, 0], spread_lane(TOPK * NT), 0.0, None, ALU.add)
                for k in range(TOPK):
                    nc.vector.tensor_copy(payload[:, k, :, 1], count_f[:, 0:NT])
                nc.vector.memset(flat[:, :, 2], 1.0)
                gflat = gate_f[:].rearrange("p k t -> p (k t)")
                for c in range(PARTS):
                    link(nc.vector.tensor_copy(flat[:, :, 3 + c], gflat))
                    if c < PARTS - 1:
                        link(tt(gflat, gflat, flat[:, :, 3 + c], ALU.subtract))
                g3 = grid.rearrange("p (j e) -> p j e", e=EXPERTS)
                link(tt(g3, spread(count_f[0:1, 0:TILES], EXPERTS),
                        tile_end[0:1, :].unsqueeze(1).broadcast_to([1, TILES, EXPERTS]), ALU.is_ge))
                link(nc.vector.tensor_reduce(experts_f[:], g3, AX.X, ALU.add))
                link(nc.vector.tensor_scalar(experts_f[:], experts_f[:], float(EXPERTS - 1), None, ALU.min))
                link(nc.vector.tensor_copy(experts[:], experts_f[:]))
                dve.sem_inc(s_place, 1)

            def spread_lane(n):
                return lane[:].broadcast_to([P, n])

            def hot(i):
                if i >= DEEP:
                    dve.wait_ge(s_slot, i - DEEP + 1)
                for k in range(TOPK):
                    nc.vector.tensor_scalar(row_hot[:, i % DEEP, k, :], count_f[:], row_f[:, k, i:i + 1], None, ALU.is_equal)
                for k in range(TOPK):
                    ins = nc.vector.tensor_scalar(col_hot[:, i % DEEP, k, :], count_f[:, 0:TILES], col_f[:, k, i:i + 1], None,
                                                  ALU.is_equal)
                link(ins)
                dve.sem_inc(s_hot, 1)
                tt(loaded[:, i % DEEP, 0], col_hot[:, i % DEEP, 0, :].unsqueeze(1).broadcast_to([P, PAYLOAD, TILES]),
                   spread(payload[:, 0, i, :], TILES), ALU.mult).then_inc(s_made, 1)

            def table():
                dve.wait_ge(s_slot, NT)
                found = found_room[:]
                link(nc.vector.tensor_copy(found, slotb[:, 0:PAYLOAD * TILES]))
                dve.sem_inc(s_ys, 1)
                col = found.rearrange("p (c n) -> p c n", c=PAYLOAD)
                link(nc.vector.scalar_tensor_tensor(out=col[:, 0], in0=col[:, 1], scalar=float(P), in1=col[:, 0],
                                                    op0=ALU.mult, op1=ALU.add))
                link(nc.vector.tensor_scalar(col[:, 2], col[:, 2], pad_minus[:], pad_row[:], ALU.mult, ALU.add))
                link(tt(col[:, 0], col[:, 0], col[:, 2], ALU.add))
                link(nc.vector.tensor_copy(ids[:], col[:, 0]))
                link(tt(col[:, 3], col[:, 3], col[:, 4], ALU.add))
                link(tt(gates[:], col[:, 3], col[:, 5], ALU.add))
                dve.sem_inc(s_table, 1)

            def do(b, kind, item):
                what = item[0]
                if what == "choose":
                    choose()
                elif what == "place":
                    place()
                elif what == "hot":
                    hot(item[1])
                elif what == "table":
                    table()
                elif what == "ids":
                    dve.wait_ge(s_scat, 16 * (tiles(b) + 1))
                    n = SHARE[kind]
                    nc.vector.tensor_copy(ids_now[:, 0:n], ids[:, bass.ds(tiles(b), n)])
                    nc.vector.tensor_copy(gates_now[:, 0:n], gates[:, bass.ds(tiles(b), n)]).then_inc(s_ids, 1)
                elif what == "query":
                    dve.wait_ge(s_q1, b + 1)
                    link(tt(qleft[:], bank_of(kind, item), qparts[:, 0, :], ALU.subtract))
                    dve.sem_inc(s_qread, 1)
                    link(nc.vector.tensor_copy(qparts[:, 1, :], qleft[:]))
                    tt(qparts[:, 2, :], qleft[:], qparts[:, 1, :], ALU.subtract).then_inc(s_q, 1)
                elif what == "keys":
                    filled(b, kind, item)
                    kv = bank_of(kind, item)[:, 0:TB * 2 * HD].rearrange("p (t e) -> p t e", t=TB)
                    nc.vector.tensor_copy(vaug[:, :, 0:HD], kv[:, :, HD:2 * HD])
                    link(nc.vector.tensor_copy(krows[:, :, 0:HD], kv[:, :, 0:HD]))
                    link(tt(kleft[:], kv[:, :, 0:HD], krows[:, :, 0:HD], ALU.subtract))
                    dve.sem_inc(s_kread, 1)
                    link(nc.vector.tensor_copy(krows[:, :, HD:2 * HD], kleft[:]))
                    link(tt(krows[:, :, 2 * HD:3 * HD], kleft[:], krows[:, :, HD:2 * HD], ALU.subtract))
                    nc.vector.tensor_copy(krows[:, :, 24:48], krows[:, :, 0:24])
                    nc.vector.tensor_copy(krows[:, :, 48:72], krows[:, :, 0:24]).then_inc(s_krows, 1)
                elif what == "a":
                    _, g, i = item
                    t, h0, n = A_BANKS[i]
                    dve.wait_ge(s_a, A_ALL * b + NA * g + i + 1)
                    keys = (t + 1) * P
                    nc.vector.tensor_reduce(nmax[:, t, HG * g + h0:HG * g + h0 + n],
                                            bank_of(kind, item)[:, 0:n * keys].rearrange("p (h s) -> p h s", h=n), AX.X,
                                            ALU.max, negate=True).then_inc(s_amax, 1)
                elif what == "split":
                    g = item[1]
                    m = nmax[:, :, HG * g:HG * g + HG]
                    dve.wait_ge(s_amax, A_ALL * b + NA * (g + 1))
                    if kind != FIRST or g:
                        dve.wait_ge(s_mT, GROUPS * b + g)
                    link(nc.vector.tensor_copy(mparts[:, :, 0, :], m))
                    link(tt(mleft[:], m, mparts[:, :, 0, :], ALU.subtract))
                    link(nc.vector.tensor_copy(mparts[:, :, 1, :], mleft[:]))
                    tt(mparts[:, :, 2, :], mleft[:], mparts[:, :, 1, :], ALU.subtract).then_inc(s_mparts, 1)
                elif what == "maxima":
                    g = item[1]
                    filled(b, kind, item)
                    if kind != FIRST or g:
                        dve.wait_ge(s_mst, 16 * (GROUPS * b + g))
                    link(nc.vector.tensor_copy(mT[:], bank16(kind, item)[0:PARTS * HG, 0:T]))
                    dve.sem_inc(s_mT, 1)
                elif what == "heads":
                    g = item[1]
                    filled(b, kind, item)
                    sums = bank_of(kind, item).rearrange("p (n r) -> p n r", r=32)
                    link(nc.vector.reciprocal(dinv[:], sums[:, :, HD]))
                    inverse = dinv[:].rearrange("p (t h) -> p t h", t=TB).unsqueeze(3).broadcast_to([P, TB, HG, HD])
                    link(tt(y[:, :, 32 * g:32 * g + 32].rearrange("p t (h d) -> p t h d", d=HD),
                            sums[:, :, 0:HD].rearrange("p (t h) d -> p t h d", t=TB), inverse, ALU.mult))
                    dve.sem_inc(s_y, 1)
                elif what == "u":
                    n = item[1]
                    if kind != FIRST or n:
                        dve.wait_ge(s_h, units(b) + n)
                    dve.wait_ge(s_th, units(b) + n + 1)
                    nc.vector.scalar_tensor_tensor(out=ga[:], in0=th[:, n % 2, :], scalar=1.0, in1=gb[:], op0=ALU.add,
                                                   op1=ALU.mult).then_inc(s_gfree, 1)
                elif what == "mul":
                    n = item[1]
                    dve.wait_ge(s_u, units(b) + n + 1)
                    dve.wait_ge(s_gfree, units(b) + n + 1)
                    if kind != FIRST or n >= 2:
                        dve.wait_ge(s_fin, units(b) + max(n - 1, 0))
                    scale = SHARED if n < FC else 1.0
                    nc.vector.scalar_tensor_tensor(out=hid[:, n % 2, :], in0=ga[:], scalar=scale, in1=ub[:], op0=ALU.mult,
                                                   op1=ALU.mult).then_inc(s_h, 1)
                elif what == "merge":
                    c = item[1]
                    dve.wait_ge(s_rl[c % 2], 16 * (c // 2 + 1))
                    rows = x_all[:, TB * c:TB * c + TB, :].rearrange("p t d -> p (t d)")
                    tt(rows, rows, rbuf[:, c % 2, :], ALU.add).then_inc(s_merged, 1)
                elif what == "out":
                    filled(b, kind, item)
                    rows = x_all[:, bass.ds(b * TB, TB), :].rearrange("p t d -> p (t d)")
                    if kind == LAST:
                        dve.wait_ge(s_merged, B)
                    tt(rows, rows, bank_of(kind, item), ALU.add).then_inc(s_res, 1)

            def sequence(b, kind):
                count["base"] = before(b, links[FIRST], links[MID]) + links["ahead"]
                count["local"] = 0
                for item in items[kind]:
                    do(b, kind, item)
                assert count["local"] == links[kind], (kind, count["local"])

            each = {"choose": 17, "place": 29, "hot": 1, "table": 7, "query": 2, "keys": 4, "split": 3, "maxima": 1, "heads": 2}
            links = {kind: sum(each.get(i[0], 0) for i in items[kind]) for kind in items}

            def moments(c):
                dve.wait_ge(s_xl[c], 16)
                for t in range(TB * c, TB * c + TB):
                    last = nc.vector.bn_stats(stats[:, t, :], x_all[:, t, :])
                link(last)
                for t in range(TB * c, TB * c + TB):
                    last = nc.vector.bn_aggr(meanvar[:, t, :], stats[:, t, :])
                link(last)
                nc.vector.tensor_scalar(vareps[:, TB * c:TB * c + TB], meanvar[:, TB * c:TB * c + TB, 1], EPS, None,
                                        ALU.add).then_inc(s_vareps, 1)

            def norm(c):
                dve.wait_ge(s_rstd, c // 2 + 1)
                for t in range(TB * c, TB * c + TB):
                    last = nc.vector.tensor_scalar(xn[:, t, :], x_all[:, t, :], meanvar[:, t, 0:1], rstd[:, t:t + 1],
                                                   ALU.subtract, ALU.mult)
                last.then_inc(s_norm, 1)

            for c in range(B + 2):
                if c < B:
                    moments(c)
                if c == 4:
                    dve.wait_ge(s_gwT, 1)
                    nc.vector.tensor_copy(gwT[:], acc[:, 0:EXPERTS]).then_inc(s_gwTs, 1)
                if c >= 2:
                    norm(c - 2)
            dve.wait_ge(s_const, 1)
            nc.vector.tensor_copy(count_f[:], count_i[:])
            link(nc.vector.tensor_copy(lane[:], lane_i[:]))
            link(nc.vector.tensor_scalar(pad_row[:], lane[:], float(PAD), None, ALU.add))
            link(nc.vector.tensor_scalar(pad_minus[:], pad_row[:], -1.0, None, ALU.mult))
            links["ahead"] = count["local"]
            sequences(dve, sequence)

        @block.gpsimd
        def _(pool):
            nc.gpsimd.memset(minus_half[:], -0.5)
            nc.gpsimd.memset(ident[:], 0.0).then_inc(s_made0, 1)
            for t in (wdown, wq, wkv, zeros):
                last = nc.gpsimd.memset(t[:], 0.0)
            last.then_inc(s_zero, 1)
            pool.wait_ge(s_made0, 1)
            nc.gpsimd.affine_select(out=ident[:], in_=ident[:], compare_op=ALU.not_equal, fill=1.0, base=0,
                                    pattern=[[-1, P]], channel_multiplier=1).then_inc(s_ident, 1)

            def power(c):
                pool.wait_ge(s_vareps, c + 2)
                both = slice(TB * c, TB * (c + 2))
                nc.gpsimd.tensor_tensor(rstd[:, both], vareps[:, both], minus_half[:, both], ALU.pow).then_inc(s_rstd, 1)

            power(0)
            for t in (never, krows, vaug):
                nc.gpsimd.memset(t[:], 0.0)
            power(2)
            nc.gpsimd.memset(earlier[:], 1.0)
            nc.gpsimd.memset(ones16[:], 1.0).then_inc(s_made0, 1)
            power(4)
            nc.gpsimd.iota(count_i[:], pattern=[[1, P]], base=0, channel_multiplier=0)
            nc.gpsimd.iota(lane_i[:], pattern=[[0, 1]], base=0, channel_multiplier=1)
            power(6)
            pool.wait_ge(s_made0, 2)
            nc.gpsimd.affine_select(out=never[:], in_=never[:], compare_op=ALU.is_ge, fill=NEVER, base=0,
                                    pattern=[[-1, P]], channel_multiplier=1)
            nc.gpsimd.affine_select(out=earlier[:], in_=earlier[:], compare_op=ALU.is_gt, fill=0.0, base=0,
                                    pattern=[[1, P]], channel_multiplier=-1)
            nc.gpsimd.memset(krows[:, :, MROW:STACKED], 1.0)
            nc.gpsimd.memset(vaug[:, :, HD:HD + 1], 1.0)
            pool.wait_ge(s_ident, 1)
            nc.gpsimd.tensor_copy(ident16[:], ident[:]).then_inc(s_const, 1)
            nc.gpsimd.memset(qst[:].rearrange("p h t -> p (h t)").bitcast(F32), 0.0).then_inc(s_zero, 1)
            rows = r_dram.rearrange("(p r) d -> p r d", p=P)
            pool.dma_start(rows, zeros[:].unsqueeze(1).broadcast_to([P, (N + P) // P, P])).then_inc(s_scat, 16)

            def gather(b, j):
                nc.gpsimd.indirect_dma_start(xs[:, j % 3, :], None, xn_dram,
                                             bass.IndirectOffsetOnAxis(ids_now[:, j:j + 1], 0)).then_inc(s_xs[j % 3], 16)

            def do(b, kind, item):
                what = item[0]
                if what == "hot":
                    i = item[1]
                    pool.wait_ge(s_hot, i + 1)
                    nc.gpsimd.tensor_tensor(loaded[:, i % DEEP, 1], col_hot[:, i % DEEP, 1, :].unsqueeze(1).broadcast_to([P, PAYLOAD, TILES]),
                                            payload[:, 1, i, :].unsqueeze(2).broadcast_to([P, PAYLOAD, TILES]),
                                            ALU.mult).then_inc(s_madep, 1)
                elif what == "ids":
                    pool.wait_ge(s_ids, b)
                    pool.sem_inc(s_apart, 1)
                    for j in range(3):
                        gather(b, j)
                elif what == "xs":
                    j = item[1] - FC
                    if j + 3 < SHARE[kind]:
                        pool.wait_ge(s_xsT, tiles(b) + j + 1)
                        pool.sem_inc(s_apart, 1)
                        gather(b, j + 3)
                elif what == "fin" and item[1] >= FC:
                    j = item[1] - FC
                    pool.wait_ge(s_ys, tiles(b) + j + 2)
                    pool.sem_inc(s_apart, 1)
                    pool.wait_ge(s_scat, 16 * (tiles(b) + j + 1))
                    pool.sem_inc(s_apart, 1)
                    nc.gpsimd.indirect_dma_start(r_dram, bass.IndirectOffsetOnAxis(ids_now[:, j:j + 1], 0), ys[:, j % 3, :],
                                                 None, compute_op=ALU.add).then_inc(s_scat, 16)

            def sequence(b, kind):
                for item in items[kind]:
                    do(b, kind, item)
                if kind == FIRST:
                    pool.wait_ge(s_xnst, 16 * (B + 1))

            sequences(pool, sequence)


_INS = ["L0_attn_x", "L0_attn_Wc_down", "L0_attn_Wq_up", "L0_attn_Wkv_up", "L0_attn_Wc_proj", "L0_ffn_gate_W",
        "L0_ffn_w1_e", "L0_ffn_w3_e", "L0_ffn_w2_e", "L0_ffn_w1_s", "L0_ffn_w3_s", "L0_ffn_w2_s"]


def kernel(**inputs):
    import numpy as _np
    import concourse.bacc as _bacc
    from concourse.bass_utils import run_bass_kernel_spmd as _run

    nc = _bacc.Bacc("TRN2", target_bir_lowering=False, num_devices=1)
    arrays, args = {}, []
    for name in _INS:
        a = _np.ascontiguousarray(inputs[name])
        arrays[f"in_{name}"] = a
        args.append(nc.dram_tensor(f"in_{name}", a.shape, mybir.dt.from_np(a.dtype), kind="ExternalInput").ap())
    shape = arrays["in_L0_attn_x"].shape
    args.append(nc.dram_tensor("out_0", shape, F32, kind="ExternalOutput").ap())
    build(nc, *args)
    r = _run(nc, [arrays], core_ids=[0])
    return r.results[0]["out_0"]
```

```python
from contextlib import ExitStack

import concourse.bass as bass
from concourse import mybir

F32 = mybir.dt.float32
BF16 = mybir.dt.bfloat16
U32 = mybir.dt.uint32
I32 = mybir.dt.int32
ALU = mybir.AluOpType
ACT = mybir.ActivationFunctionType
AX = mybir.AxisListType

P = 128
D = 128
LAT = 64
HEADS, HD = 16, 8
GROUPS = 4
HG = HEADS // GROUPS
TB = 4
T = TB * P
B = 8
NT = B * TB
N = NT * P
EXPERTS, TOPK = 8, 2
F = 512
FC = F // P
EPS = 1e-5
SCALE = HD ** -0.5
NEVER = -3.0e38
ROUTED = 0.5 * 0.5
SHARED = 0.5 * 0.5 / 8

TILES = N * TOPK // P + EXPERTS
MIDDLE = B - 2
PER = 10
REST = TILES - PER * MIDDLE
assert REST > 0
PAD = N

PARTS = 3
MROW = 96
STACKED = MROW + PARTS
PAYLOAD = 3 + PARTS

PCOL = {0: 0, 1: 512, 3: 896, 2: 1024}
PCOLS = 1280

SIDE = EXPERTS + 2 * HD

A_BANKS = [(3, 0, 1), (3, 1, 1), (3, 2, 1), (3, 3, 1), (2, 0, 1), (2, 1, 1), (2, 2, 1), (2, 3, 1),
           (1, 0, 2), (1, 2, 2), (0, 0, 4)]
B_BANKS = [(h, 1, (0,)) for h in range(HG)] + [(h, 1, (1, 3)) for h in range(HG)] + [(0, 2, (2,)), (2, 2, (2,))]
NA, NB = len(A_BANKS), len(B_BANKS)
RING = 4
DEEP = 3
A_ALL, B_ALL = GROUPS * NA, GROUPS * NB

FIRST, MID, LAST = "first", "middle", "last"
QUERY = ("query",)
SHARE = {FIRST: 0, MID: PER, LAST: REST}
UNITS = {kind: FC + SHARE[kind] for kind in SHARE}


COMMON = dict(ids=5, query=0.5, keys=2, kstack=6, split=0.9, yturn=2, project=4,
              v_a=0.3, v_turns=0.5, v_units=0, a_b=0.3, a_units=0.5, a_turns=0.5)
PACE = {
    FIRST: COMMON | dict(kstack=1, first=11, group=10.5, turn=12, b=19.26, pv=32.5, heads=34.16, early=2, end=78,
                         prefix=8, slots=12, slot=2, lag=1.5),
    MID: COMMON | dict(ids=4, first=11, group=12, turn=13.5, b=22.5, pv=36.5, heads=39, early=4, end=92),
    LAST: COMMON | dict(query=-0.08, kstack=5.15, yturn=1.32, v_units=-0.07, first=11, group=10.97, turn=12.5, b=20,
                        pv=32, heads=34.5, early=4, end=63.21, merge=78, each=0.5),
}
LATER = {"vector": {"a": "v_a", "split": "v_a", "query": "v_turns", "keys": "v_turns", "maxima": "v_turns",
                    "heads": "v_turns", "out": "v_turns", "u": "v_units", "mul": "v_units"},
         "scalar": {"b": "a_b", "g": "a_units", "fin": "a_units", "xs": "a_turns",
                    "query": "a_turns", "kstack": "a_turns", "turn": "a_turns", "pv": "a_turns"}}


def plan(kind, engine=None):
    pace = PACE[kind]
    later = LATER.get(engine, {})
    at = []

    def put(time, *item):
        at.append((time + (pace[later[item[0]]] if item[0] in later else 0), len(at), item))

    put(pace["query"], "query")
    put(pace["keys"], "keys")
    put(pace["kstack"], "kstack")
    for g in range(GROUPS):
        start = pace["first"] + pace["group"] * g
        for i in range(NA):
            put(start + pace["group"] * i / NA, "a", g, i)
        put(start + pace["group"] * (NA - 1) / NA + pace["split"], "split", g)
        put(start + pace["turn"], "maxima", g)
        for i in range(NB):
            put(start + pace["b"] + pace["group"] * i / NB, "b", g, i)
        put(start + pace["pv"], "pv", g)
        put(start + pace["heads"], "heads", g)
    last = pace["first"] + pace["group"] * (GROUPS - 1) + pace["heads"]
    put(last + pace["yturn"], "turn")
    put(last + pace["project"], "project")
    put(last + pace["project"] + 0.1, "out")
    units, early = UNITS[kind], pace["early"]

    def due(n):
        return (pace["first"] * n / early if n <= early else
                pace["first"] + (pace["end"] - pace["first"]) * (n - early) / (units - early))

    for n in range(units):
        span = due(n + 1) - due(n)
        put(due(n), "g", n)
        if n + 1 >= FC and n + 1 < units:
            put(due(n) + 0.25 * span, "xs", n + 1)
        put(due(n) + 0.5 * span, "u", n)
        if n:
            put(due(n) + 0.75 * span, "fin", n - 1)
        put(due(n) + 0.8 * span, "mul", n)
    put(due(units) - 0.6, "fin", units - 1)
    if kind == FIRST:
        put(pace["keys"] + 1, "choose")
        put(pace["prefix"], "prefix")
        put(pace["prefix"] + 0.1, "place")
        for i in range(NT):
            put(pace["slots"] + pace["slot"] * i, "hot", i)
            put(pace["slots"] + pace["slot"] * (i + pace["lag"]), "slot", i)
        put(pace["slots"] + pace["slot"] * (NT + 2), "table")
    else:
        put(pace["ids"], "ids")
    if kind == LAST:
        for c in range(B):
            put(pace["merge"] + pace["each"] * c, "merge", c)
    return [item for _, _, item in sorted(at)]


def in_turn(item):
    return item[0] in ("query", "kstack", "maxima", "heads", "turn")


def in_ring(item):
    return item[0] in ("a", "b", "pv") or in_turn(item)


def places(items, wanted):
    return {item: n for n, item in enumerate(i for i in items if wanted(i))}


def before(b, first, each):
    return 0 if isinstance(b, int) and b == 0 else each * b + (first - each)


def sequences(eng, run):
    run(0, FIRST)
    with eng.Fori(1, B - 1) as b:
        run(b, MID)
    run(B - 1, LAST)


def build(nc, x, Wc_down, Wq_up, Wkv_up, Wc_proj, gate_W, w1_e, w3_e, w2_e, w1_s, w3_s, w2_s, out):
    items = {kind: plan(kind) for kind in (FIRST, MID, LAST)}
    vector_items = {kind: plan(kind, "vector") for kind in items}
    scalar_items = {kind: plan(kind, "scalar") for kind in items}
    turn_at = {kind: places(items[kind], in_turn) for kind in items}
    TURNS = len(turn_at[MID])
    ring_items = {kind: [i for i in items[kind] if in_ring(i)] for kind in items}
    ring_at = {kind: places(items[kind], in_ring) for kind in items}
    assert ring_items[FIRST][-RING:] == ring_items[MID][-RING:]

    with ExitStack() as ctx:
        def sb(name, shape, dt=F32):
            return ctx.enter_context(nc.sbuf_tensor(name, shape, dt))

        def bank(name, shape):
            return ctx.enter_context(nc.psum_tensor(name, shape, F32))

        def sem(name):
            return ctx.enter_context(nc.semaphore(name))

        ring = bank("ring", [P, RING, 512])
        gb = bank("gb", [P, 512])
        ub = bank("ub", [P, 512])
        acc = bank("acc", [P, 512])
        slotb = bank("slotb", [P, 512])

        w13 = sb("w13", [P, 1 + EXPERTS, 2, F])
        w1, w3 = w13[:, :, 0, :], w13[:, :, 1, :]
        w2 = sb("w2", [P, 1 + EXPERTS, FC, D])
        w13_now = sb("w13_now", [P, 2, 2, F])
        w2_now = sb("w2_now", [P, 2, FC, D])
        wdown = sb("wdown", [P, P])
        wq = sb("wq", [P, P])
        wkv = sb("wkv", [P, 2 * HD])
        wdownT = sb("wdownT", [P, P])
        wxq = sb("wxq", [P, P])
        wproj = sb("wproj", [P, D])
        gw = sb("gw", [EXPERTS, D])
        wside = sb("wside", [P, SIDE])
        side = sb("side", [P, NT, SIDE])
        ident = sb("ident", [P, P])
        ident16 = sb("ident16", [P, P], BF16)
        never = sb("never", [P, P], BF16)
        earlier = sb("earlier", [P, P], BF16)
        ones16 = sb("ones16", [P, P], BF16)
        count_i = sb("count_i", [P, P], I32)
        count_f = sb("count_f", [P, P])
        lane_i = sb("lane_i", [P, 1], I32)
        lane = sb("lane", [P, 1])
        pad_row = sb("pad_row", [P, 1])
        pad_minus = sb("pad_minus", [P, 1])
        minus_half = sb("minus_half", [P, NT])
        zeros = sb("zeros", [P, P])
        x_all = sb("x_all", [P, NT, D])
        xnT = sb("xnT", [P, N])
        stats = sb("stats", [P, NT, 6])
        meanvar = sb("meanvar", [P, NT, 2])
        vareps = sb("vareps", [P, NT])
        rstd = sb("rstd", [P, NT])
        lmax = sb("lmax", [P, NT])
        linv = sb("linv", [P, NT])
        best = sb("best", [P, TOPK, NT])
        rank1 = sb("rank1", [P, NT])
        tiles_of = sb("tiles_of", [P, EXPERTS])
        tile_end = sb("tile_end", [P, EXPERTS])
        tile_begin = sb("tile_begin", [P, EXPERTS])
        slot_f = sb("slot_f", [P, TOPK, NT])
        slot_i = sb("slot_i", [P, TOPK, NT], I32)
        row_i = sb("row_i", [P, TOPK, NT], I32)
        col_f = sb("col_f", [P, TOPK, NT])
        row_f = sb("row_f", [P, TOPK, NT])
        gate_f = sb("gate_f", [P, TOPK, NT])
        payload = sb("payload", [P, TOPK, NT, PAYLOAD], BF16)
        row_hot = sb("row_hot", [P, DEEP, TOPK, P], BF16)
        col_hot = sb("col_hot", [P, DEEP, TOPK, TILES], BF16)
        loaded = sb("loaded", [P, DEEP, TOPK, PAYLOAD, TILES], BF16)
        ids = sb("ids", [P, TILES], U32)
        gates = sb("gates", [P, TILES])
        experts_f = sb("experts_f", [1, TILES])
        experts = sb("experts", [1, TILES], I32)
        ids_now = sb("ids_now", [P, max(SHARE.values())], U32)
        gates_now = sb("gates_now", [P, max(SHARE.values())])
        qparts = sb("qparts", [P, PARTS, T], BF16)
        qleft = sb("qleft", [P, T])
        qst = sb("qst", [P, HEADS, T], BF16)
        kleft = sb("kleft", [P, TB, HD])
        krows = sb("krows", [P, TB, P], BF16)
        kst = sb("kst", [P, T], BF16)
        vaug = sb("vaug", [P, TB, 32])
        nmax = sb("nmax", [P, TB, HEADS])
        mleft = sb("mleft", [P, TB, HG])
        mparts = sb("mparts", [P, TB, PARTS, HG], BF16)
        mT = sb("mT", [PARTS * HG, T], BF16)
        probT = sb("probT", [P, 2, HG, PCOLS])
        hraw = sb("hraw", [P, T])
        dinv = sb("dinv", [P, TB * HG])
        y = sb("y", [P, TB, D])
        yT = sb("yT", [P, T])
        xs = sb("xs", [P, 3, D])
        xsT = sb("xsT", [P, 2, P])
        th = sb("th", [P, 2, F])
        ga = sb("ga", [P, F])
        hid = sb("hid", [P, 2, F])
        ys = sb("ys", [P, 3, D])
        found_room = sb("found", [P, PAYLOAD * TILES])

        spare = probT[:].rearrange("p a h c -> p (a h c)")
        xn = spare[:, 0:N].rearrange("p (t d) -> p t d", d=D)
        NE = NT * EXPERTS
        room = [spare[:, N + NE * i:N + NE * (i + 1)] for i in range(14)]
        (lshift, lexp, probs, same, first, probs2, second, weight, cumul, rank, thresh, restart, picked,
         mask_room) = room
        mask16 = mask_room.bitcast(BF16)[:, 0:NE]
        grid = spare[0:1, N + 14 * NE:N + 14 * NE + TILES * EXPERTS]

        def rbuf(c):
            if c < B - 1:
                return xnT[:, c * T:(c + 1) * T]
            return loaded[:].rearrange("p i k c n -> p (i k c n)").bitcast(F32)[:, 0:T]

        assert N + 14 * NE + TILES * EXPERTS <= 2 * HG * PCOLS

        q_dram = nc.dram_tensor("q_scratch", (PARTS, HEADS, HD, T), BF16, kind="Internal").ap()
        m_dram = nc.dram_tensor("m_scratch", (GROUPS, PARTS, HG, T), BF16, kind="Internal").ap()
        xn_dram = nc.dram_tensor("xn_scratch", (N + P, D), F32, kind="Internal").ap()
        r_dram = nc.dram_tensor("routed_scratch", (N + P, D), F32, kind="Internal").ap()

        s_w = [sem(f"weights_loaded_{e}") for e in range(1 + EXPERTS)]
        s_small = sem("small_weights_loaded")
        s_gw = sem("gate_weights_loaded")
        s_zero = sem("buffers_zeroed")
        s_const = sem("constants_made")
        s_gwT = sem("gate_weights_turned")
        s_gwTs = sem("gate_weights_saved")
        s_xl = [sem(f"x_loaded_{c}") for c in range(B)]
        s_vareps = sem("variance_ready")
        s_rstd = sem("rstd_ready")
        s_norm = sem("normed")
        s_xnst = sem("xn_stored")
        s_turn = sem("x_turned")
        s_xnT = sem("xnT_ready")
        s_logits = sem("logits_and_keys_ready")
        s_side = sem("logits_and_keys_saved")
        s_lread = sem("logits_shifted")
        s_lexp = sem("logits_exped")
        s_mask = sem("choices_ready")
        s_prefix = sem("ranks_counted")
        s_spare = sem("routing_done_with_room")
        s_place = sem("places_ready")
        s_hot = sem("one_hot_tiles_ready")
        s_made0 = sem("constants_begun")
        s_ident = sem("identity_made")
        s_made = sem("slot_operands_made_vector")
        s_madep = sem("slot_operands_made_pool")
        s_slot = sem("slots_added")
        s_table = sem("table_ready")
        s_ids = sem("ids_ready")
        s_wprod = sem("weight_products_made")
        s_wsave = sem("weight_products_saved")
        s_q1 = sem("query_first_part")
        s_qread = sem("query_read")
        s_q = sem("query_parts_ready")
        s_qst0 = sem("query_parts_stored")
        s_qst = sem("query_stack_loaded")
        s_krows = sem("key_rows_ready")
        s_kst = sem("key_stack_ready")
        s_a = sem("a_scored")
        s_amax = sem("a_maxed")
        s_mparts = sem("maxima_parts_ready")
        s_mT = sem("maxima_turned")
        s_mst = sem("maxima_stored")
        s_m = [sem(f"maxima_loaded_{g}") for g in range(GROUPS)]
        s_b = sem("b_scored")
        s_exp = sem("b_exped")
        s_pv = sem("heads_summed")
        s_hraw = sem("heads_saved")
        s_y = sem("heads_normed")
        s_yT = sem("yT_ready")
        s_misc = sem("turned_or_product_in_ring")
        s_xs = [sem(f"slot_rows_gathered_{k}") for k in range(3)]
        s_xt = sem("slot_rows_turning")
        s_xsT = sem("slot_rows_turned")
        s_g = sem("g_ready")
        s_th = sem("tanh_done")
        s_gfree = sem("g_read")
        s_u = sem("u_ready")
        s_h = sem("hidden_ready")
        s_fin = sem("units_finished")
        s_w13 = [sem(f"expert_in_weights_staged_{k}") for k in range(2)]
        s_w2 = [sem(f"expert_out_weights_staged_{k}") for k in range(2)]
        s_ys = sem("slot_result_ready")
        s_scat = sem("routed_rows_added")
        s_accfull = sem("acc_ready")
        s_res = sem("result_ready")
        s_rl = [sem(f"routed_rows_loaded_{k}") for k in range(B)]
        s_merged = sem("merged")
        s_out = sem("result_stored")
        s_dve = sem("vector_step")
        s_apart = sem("waits_carried")

        def turns(b, kind, item):
            return TURNS * b + turn_at[kind][item] + 1

        def units(b):
            return before(b, UNITS[FIRST], UNITS[MID])

        def tiles(b):
            return PER * b - PER

        def staged(b, j):
            return 16 * (((PER + 1 - j % 2) // 2) * (b - 1) + j // 2 + 1)

        def gathered(b, j):
            return 16 * (((PER + 2 - j % 3) // 3) * (b - 1) + j // 3 + 1)

        def bank_of(kind, item):
            return ring[:, ring_at[kind][item] % RING, :]

        def bank16(kind, item):
            return bank_of(kind, item).bitcast(BF16)

        def read(b, item):
            what, g = item[0], item[1] if len(item) > 1 else 0
            return {"query": (s_qread, b + 1),
                    "kstack": (s_kst, b + 1), "maxima": (s_mT, GROUPS * b + g + 1), "heads": (s_y, GROUPS * b + g + 1),
                    "turn": (s_yT, b + 1), "pv": (s_hraw, GROUPS * b + g + 1),
                    "a": (s_amax, A_ALL * b + NA * g + item[-1] + 1 if what == "a" else 0),
                    "b": (s_exp, B_ALL * b + NB * g + item[-1] + 1 if what == "b" else 0)}[what]

        block = ctx.enter_context(nc.Block())

        @block.sync
        def _(sp):
            x_tiles = x.rearrange("b (t p) d -> b p t d", p=P)
            out_tiles = out.rearrange("b (t p) d -> b p t d", p=P)
            for c in range(B):
                sp.dma_start(x_all[:, TB * c:TB * c + TB, :], x_tiles[c]).then_inc(s_xl[c], 16)
                if c == 0:
                    sp.dma_start(gw[:], gate_W).then_inc(s_gw, 16)
            for c in range(B):
                sp.wait_ge(s_norm, c + 1)
                rows = xn_dram[c * T:(c + 1) * T, :].rearrange("(t p) d -> p t d", p=P)
                sp.dma_start(rows, xn[:, TB * c:TB * c + TB, :]).then_inc(s_xnst, 16)
            sp.dma_start(xn_dram[N:N + P, :], zeros[:]).then_inc(s_xnst, 16)
            def wait(s, n):
                sp.wait_ge(s, n)
                sp.sem_inc(s_apart, 1)

            def stage_in(b, j):
                wait(s_u, units(b) + (FC + j - 1 if j >= 2 else 0))
                e = sp.value_load(experts[0:1, bass.ds(tiles(b) + j, 1)], min_val=0, max_val=EXPERTS - 1)
                sp.dma_start(w13_now[:, j % 2], w13[:, e + 1]).then_inc(s_w13[j % 2], 16)
                return e

            def stage_out(b, j, e):
                wait(s_fin, units(b) + (FC + j - 1 if j >= 2 else 0))
                sp.dma_start(w2_now[:, j % 2], w2[:, e + 1]).then_inc(s_w2[j % 2], 16)

            def do(b, kind, item):
                what = item[0]
                if what == "query" and kind != FIRST:
                    for j in range(2):
                        expert[j] = stage_in(b, j)
                if what == "query":
                    wait(s_q, b + 1)
                    sp.dma_start(q_dram.rearrange("i h d t -> (h d) i t"), qparts[:]).then_inc(s_qst0, 16)
                    wait(s_qst0, 16 * (b + 1))
                    if kind != FIRST:
                        wait(s_b, B_ALL * b)
                    else:
                        wait(s_zero, 2)
                    for i in range(PARTS):
                        for j in range(PARTS):
                            row = (i * PARTS + j) * HD
                            sp.dma_start(qst[row:row + HD, :, :], q_dram[i].rearrange("h d t -> d h t")).then_inc(s_qst, 16)
                    if kind == FIRST:
                        for e in range(EXPERTS):
                            sp.dma_start(w1[:, 1 + e, :], w1_e[e]).then_inc(s_w[1 + e], 16)
                            sp.dma_start(w3[:, 1 + e, :], w3_e[e]).then_inc(s_w[1 + e], 16)
                            sp.dma_start(w2[:, 1 + e, :, :], w2_e[e].rearrange("(c p) d -> p c d", p=P)).then_inc(s_w[1 + e], 16)
                    else:
                        for j in range(2):
                            stage_out(b, j, expert[j])
                elif what == "u" and item[1] >= FC:
                    j = item[1] - FC
                    if j + 2 < SHARE[kind]:
                        expert[j % 2] = stage_in(b, j + 2)
                elif what == "fin" and item[1] >= FC:
                    j = item[1] - FC
                    if j + 2 < SHARE[kind]:
                        stage_out(b, j + 2, expert[j % 2])
                elif what == "maxima":
                    g = item[1]
                    wait(s_mT, GROUPS * b + g + 1)
                    sp.dma_start(m_dram[g].rearrange("i h t -> (i h) t"), mT[:]).then_inc(s_mst, 16)
                    wait(s_mst, 16 * (GROUPS * b + g + 1))
                    sp.dma_start(qst[MROW:STACKED, HG * g:HG * g + HG, :], m_dram[g]).then_inc(s_m[g], 16)

            expert = [None, None]

            def sequence(b, kind):
                for item in items[kind]:
                    do(b, kind, item)
                if kind == FIRST:
                    for e in range(1, 1 + EXPERTS):
                        sp.wait_ge(s_w[e], 48)
                    sp.wait_ge(s_table, 1)
                if kind == LAST:
                    sp.wait_ge(s_scat, 16 * (1 + TILES))
                    for c in range(B):
                        rows = r_dram[c * T:(c + 1) * T, :].rearrange("(t p) d -> p t d", p=P)
                        sp.dma_start(rbuf(c).rearrange("p (t d) -> p t d", d=D), rows).then_inc(s_rl[c], 16)
                    for c in range(B - 1):
                        sp.wait_ge(s_merged, c + 1)
                        sp.dma_start(out_tiles[c], x_all[:, TB * c:TB * (c + 1), :]).then_inc(s_out, 16)
                    sp.wait_ge(s_res, B)
                    sp.dma_start(out_tiles[B - 1], x_all[:, TB * (B - 1):TB * B, :]).then_inc(s_out, 16)

            sequences(sp, sequence)
            sp.wait_ge(s_out, 16 * B)

        @block.tensor
        def _(pe):
            def transposes(of, eye, where, done):
                for t in range(TB):
                    last = nc.tensor.transpose(where(t), of(t), eye)
                last.then_inc(done, 1)

            def do(b, kind, item):
                what = item[0]
                if in_ring(item):
                    k = ring_at[kind][item]
                    o = bank_of(kind, item)
                    if k >= RING:
                        pe.wait_ge(*read(b, ring_items[kind][k - RING]))
                    elif kind != FIRST:
                        past = [n for n in range(len(ring_items[MID])) if n % RING == k][-1]
                        pe.wait_ge(*read(b - 1, ring_items[MID][past]))
                if what == "query":
                    nc.tensor.matmul(o, wxq[:], xnT[:, bass.ds(b * T, T)], start=True, stop=True).then_inc(s_misc, 1)
                elif what == "kstack":
                    pe.wait_ge(s_krows, b + 1)
                    transposes(lambda t: krows[:, t, :], ident16[:], lambda t: bank16(kind, item)[:, t * P:(t + 1) * P], s_misc)
                elif what in ("a", "b"):
                    if what == "a":
                        scores_a(b, kind, item)
                    else:
                        scores_b(b, kind, item)
                elif what == "maxima":
                    pe.wait_ge(s_mparts, GROUPS * b + item[1] + 1)
                    transposes(lambda t: mparts[:, t].rearrange("p i h -> p (i h)"), ident16[:],
                               lambda t: bank16(kind, item)[0:PARTS * HG, t * P:(t + 1) * P], s_misc)
                elif what == "pv":
                    pv(b, item[1], o)
                elif what == "heads":
                    pe.wait_ge(s_hraw, GROUPS * b + item[1] + 1)
                    transposes(lambda t: hraw[:, t * P:(t + 1) * P], ident[:], lambda t: o[:, t * P:(t + 1) * P], s_misc)
                elif what == "turn":
                    pe.wait_ge(s_y, GROUPS * (b + 1))
                    transposes(lambda t: y[:, t, :], ident[:], lambda t: o[:, t * P:(t + 1) * P], s_misc)
                elif what == "project":
                    pe.wait_ge(s_yT, b + 1)
                    assert items[kind].index(item) > items[kind].index(("fin", FC - 1))
                    for t in range(TB):
                        last = nc.tensor.matmul(acc[:, t * D:(t + 1) * D], yT[:, t * P:(t + 1) * P], wproj[:], start=False,
                                                stop=True, skip_group_check=True)
                    last.then_inc(s_accfull, 1)
                elif what == "g":
                    n = item[1]
                    pe_wait(s_gfree, units(b) + n)
                    if n < FC:
                        nc.tensor.matmul(gb[:], w1[:, 0, n * P:(n + 1) * P], xnT[:, bass.ds(b * T, T)], start=True,
                                         stop=True).then_inc(s_g, 1)
                    else:
                        j = n - FC
                        pe.wait_ge(s_xsT, tiles(b) + j + 1)
                        pe.wait_ge(s_w13[j % 2], staged(b, j))
                        expert_product(gb, 0, j, s_g)
                elif what == "u":
                    n = item[1]
                    pe_wait(s_h, units(b) + n)
                    if n < FC:
                        nc.tensor.matmul(ub[:], w3[:, 0, n * P:(n + 1) * P], xnT[:, bass.ds(b * T, T)], start=True,
                                         stop=True).then_inc(s_u, 1)
                    else:
                        j = n - FC
                        expert_product(ub, 1, j, s_u)
                elif what == "xs":
                    j = item[1] - FC
                    pe.wait_ge(s_ys, tiles(b) + slot_uses(kind, item, "fin") + 1)
                    pe.wait_ge(s_xs[j % 3], gathered(b, j))
                    nc.tensor.transpose(slotb[:, 0:P], xs[:, j % 3, :], ident[:]).then_inc(s_xt, 1)
                elif what == "fin":
                    n = item[1]
                    pe.wait_ge(s_h, units(b) + n + 1)
                    if n < FC:
                        if n == 0:
                            if kind != FIRST:
                                pe.wait_ge(s_res, b)
                        for t in range(TB):
                            ins = nc.tensor.matmul(acc[:, t * D:(t + 1) * D], hid[:, n % 2, t * P:(t + 1) * P], w2[:, 0, n, :],
                                                   start=(n == 0 and t == 0), stop=False, skip_group_check=True)
                        ins.then_inc(s_fin, 1)
                    else:
                        j = n - FC
                        pe.wait_ge(s_w2[j % 2], staged(b, j))
                        pe.wait_ge(s_xsT, tiles(b) + slot_uses(kind, item, "xs"))
                        if n < FC + 1 or slot_order(kind)[slot_order(kind).index(item) - 1][0] == "fin":
                            pe.wait_ge(s_ys, tiles(b) + j + 1)
                        for c in range(FC):
                            last = nc.tensor.matmul(slotb[:, 0:D], hid[:, n % 2, c * P:(c + 1) * P], w2_now[:, j % 2, c, :],
                                                    start=(c == 0), stop=(c == FC - 1))
                        last.then_inc(s_fin, 1)
                elif what == "prefix":
                    pe.wait_ge(s_mask, 1)
                    nc.tensor.matmul(slotb[:, 0:NE], earlier[:], mask16, start=True, stop=True, skip_group_check=True)
                    nc.tensor.matmul(slotb[:, NE:2 * NE], ones16[:], mask16, start=False, stop=True,
                                     skip_group_check=True).then_inc(s_prefix, 1)
                elif what == "slot":
                    i = item[1]
                    if i == 0:
                        pe.wait_ge(s_spare, 1)
                    pe.wait_ge(s_made, i + 1)
                    pe.wait_ge(s_madep, i + 1)
                    for k in range(TOPK):
                        ins = nc.tensor.matmul(slotb[:, 0:PAYLOAD * TILES], row_hot[:, i % DEEP, k, :],
                                               loaded[:, i % DEEP, k].rearrange("p c n -> p (c n)"),
                                               start=(i == 0 and k == 0), stop=(i == NT - 1 and k == TOPK - 1))
                    ins.then_inc(s_slot, 1)

            def expert_product(o, which, j, done):
                for c in range(FC):
                    last = nc.tensor.matmul(o[:, c * P:(c + 1) * P], w13_now[:, j % 2, which, c * P:(c + 1) * P],
                                            xsT[:, j % 2, :], start=(c == 0), stop=True, skip_group_check=True)
                last.then_inc(done, 1)

            def slot_order(kind):
                return [i for i in items[kind] if i[0] == "xs" or (i[0] == "fin" and i[1] >= FC)]

            def slot_uses(kind, item, what):
                order = slot_order(kind)
                return sum(i[0] == what for i in order[:order.index(item)])

            def pe_wait(s, n):
                if not (isinstance(n, int) and n == 0):
                    pe.wait_ge(s, n)

            def scores_a(b, kind, item):
                _, g, i = item
                t, h0, n = A_BANKS[i]
                if (g, i) == (0, 0):
                    pe.wait_ge(s_qst, 16 * PARTS * PARTS * (b + 1))
                    pe.wait_ge(s_kst, b + 1)
                keys = (t + 1) * P
                o = bank_of(kind, item)
                for h in range(n):
                    nc.tensor.matmul(o[:, h * keys:(h + 1) * keys], qst[0:MROW, HG * g + h0 + h, t * P:(t + 1) * P],
                                     kst[0:MROW, 0:keys], start=(h == 0), stop=False, skip_group_check=True)
                diagonal = o[:, 0:n * keys].rearrange("p (h s) -> p h s", h=n)[:, :, t * P:keys]
                nc.tensor.matmul(diagonal, ident16[:], never[:].unsqueeze(1).broadcast_to([P, n, P]), start=False,
                                 stop=True, skip_group_check=True).then_inc(s_a, 1)

            def scores_b(b, kind, item):
                _, g, i = item
                h0, n, key_tiles = B_BANKS[i]
                if i == 0:
                    pe.wait_ge(s_m[g], 16 * (b + 1))
                o = bank_of(kind, item)
                col = 0
                for h in range(h0, h0 + n):
                    for s in key_tiles:
                        w = T - s * P
                        nc.tensor.matmul(o[:, col:col + w], kst[0:STACKED, s * P:(s + 1) * P],
                                         qst[0:STACKED, HG * g + h, s * P:T], start=(col == 0), stop=False,
                                         skip_group_check=True)
                        col += w
                if len(key_tiles) * n == 1:
                    diagonal, eye = o[:, 0:P], ident16[:]
                else:
                    eye = ident16[:].unsqueeze(1).broadcast_to([P, 2, P])
                    diagonal = (o.rearrange("p (c w) -> p c w", w=P)[:, 0:4:3, :] if n == 1 else
                                o.rearrange("p (n c) -> p n c", n=2)[:, :, 0:P])
                nc.tensor.matmul(diagonal, never[:], eye, start=False, stop=True, skip_group_check=True).then_inc(s_b, 1)

            def pv(b, g, o):
                pe.wait_ge(s_exp, B_ALL * b + NB * (g + 1))
                for s in range(TB):
                    for h in range(HG):
                        c = PCOL[s]
                        last = nc.tensor.matmul(o[32 * h:32 * h + 32, s * P:T], vaug[:, s, :],
                                                probT[:, g % 2, h, c:c + T - s * P], start=(s == 0),
                                                stop=(s == TB - 1), skip_group_check=True)
                last.then_inc(s_pv, 1)

            pe.wait_ge(s_ident, 1)
            pe.wait_ge(s_gw, 16)
            nc.tensor.transpose(acc[:, 0:EXPERTS], gw[:], ident[0:EXPERTS, 0:EXPERTS]).then_inc(s_gwT, 1)

            pe.wait_ge(s_small, 16 * 4)
            pe.wait_ge(s_gwTs, 1)
            nc.tensor.transpose(acc[:, 0:P], wdown[:], ident[:]).then_inc(s_wprod, 1)
            pe.wait_ge(s_wsave, 1)
            nc.tensor.matmul(acc[:, 0:P], wdownT[:], wq[:], start=True, stop=True, skip_group_check=True)
            nc.tensor.matmul(acc[:, P:P + 2 * HD], wdownT[:], wkv[:], start=False, stop=True,
                             skip_group_check=True).then_inc(s_wprod, 1)

            def narrow(c):
                pe.wait_ge(s_xnT, c + 1)
                if c == 0:
                    pe.wait_ge(s_wsave, 2)
                if c >= 2:
                    pe.wait_ge(s_side, c - 1)
                for t in range(TB):
                    last = nc.tensor.matmul(ring[:, 2 + c % 2, t * SIDE:(t + 1) * SIDE],
                                            xnT[:, (TB * c + t) * P:(TB * c + t + 1) * P], wside[:], start=(t == 0),
                                            stop=True, skip_group_check=True)
                last.then_inc(s_logits, 1)

            for c in range(B):
                pe.wait_ge(s_norm, c + 1)
                if c >= 2:
                    pe.wait_ge(s_xnT, c - 1)
                transposes(lambda t: xn[:, TB * c + t, :], ident[:],
                           lambda t: (gb, ub)[c % 2][:, t * P:(t + 1) * P], s_turn)
                if c:
                    narrow(c - 1)
                if c == 1:
                    do(0, FIRST, QUERY)
            narrow(B - 1)
            pe.wait_ge(s_side, B)

            def sequence(b, kind):
                if kind == FIRST:
                    pe.wait_ge(s_w[0], 48)
                    pe.wait_ge(s_const, 1)
                for item in items[kind]:
                    if not (kind == FIRST and item == QUERY):
                        do(b, kind, item)

            sequences(pe, sequence)

        @block.scalar
        def _(act):
            act.wait_ge(s_zero, 1)
            act.dma_start(wdown[:, 0:LAT], Wc_down).then_inc(s_small, 16)
            act.dma_start(wq[0:LAT, :], Wq_up).then_inc(s_small, 16)
            act.dma_start(wkv[0:LAT, :], Wkv_up).then_inc(s_small, 16)
            act.dma_start(wproj[:], Wc_proj).then_inc(s_small, 16)
            act.dma_start(w1[:, 0, :].rearrange("p (n f) -> p n f", n=8), w1_s.rearrange("n d f -> d n f")).then_inc(s_w[0], 16)
            act.dma_start(w3[:, 0, :].rearrange("p (n f) -> p n f", n=8), w3_s.rearrange("n d f -> d n f")).then_inc(s_w[0], 16)
            act.dma_start(w2[:, 0, :, :], w2_s.rearrange("n f d -> (n f) d").rearrange("(c p) d -> p c d", p=P)).then_inc(s_w[0], 16)
            def filled(b, kind, item):
                act.wait_ge(s_misc, turns(b, kind, item))

            def do(b, kind, item):
                what = item[0]
                if what == "choose":
                    act.wait_ge(s_lread, 1)
                    nc.scalar.activation(lexp, lshift, ACT.Exp).then_inc(s_lexp, 1)
                elif what == "query":
                    filled(b, kind, item)
                    if kind != FIRST:
                        act.wait_ge(s_qst0, 16 * b)
                    nc.scalar.copy(qparts[:, 0, :], bank_of(kind, item)).then_inc(s_q1, 1)
                elif what == "kstack":
                    filled(b, kind, item)
                    nc.scalar.copy(kst[:], bank16(kind, item)[:, 0:T]).then_inc(s_kst, 1)
                elif what == "b":
                    _, g, i = item
                    h0, n, key_tiles = B_BANKS[i]
                    act.wait_ge(s_b, B_ALL * b + NB * g + i + 1)
                    if i == 0:
                        if kind == FIRST and g == 0:
                            act.wait_ge(s_place, 1)
                            act.wait_ge(s_xnst, 16 * (B + 1))
                        if kind != FIRST or g >= 2:
                            act.wait_ge(s_pv, GROUPS * b + max(g - 1, 0))
                    c = PCOL[key_tiles[0]]
                    w = sum(T - s * P for s in key_tiles)
                    nc.scalar.activation(probT[:, g % 2, h0:h0 + n, c:c + w],
                                         bank_of(kind, item).rearrange("p (h c) -> p h c", h=n), ACT.Exp,
                                         scale=SCALE).then_inc(s_exp, 1)
                elif what == "pv":
                    g = item[1]
                    act.wait_ge(s_pv, GROUPS * b + g + 1)
                    if g:
                        act.wait_ge(s_misc, turns(b, kind, ("heads", g - 1)))
                    nc.scalar.copy(hraw[:], bank_of(kind, item)).then_inc(s_hraw, 1)
                elif what == "turn":
                    filled(b, kind, item)
                    nc.scalar.copy(yT[:], bank_of(kind, item)).then_inc(s_yT, 1)
                elif what == "g":
                    n = item[1]
                    act.wait_ge(s_g, units(b) + n + 1)
                    if kind != FIRST or n >= 2:
                        act.wait_ge(s_gfree, units(b) + max(n - 1, 0))
                    nc.scalar.activation(th[:, n % 2, :], gb[:], ACT.Tanh, scale=0.5).then_inc(s_th, 1)
                elif what == "xs":
                    j = item[1] - FC
                    act.wait_ge(s_xt, tiles(b) + j + 1)
                    act.wait_ge(s_u, units(b) + (item[1] - 1 if j >= 2 else 0))
                    nc.scalar.copy(xsT[:, j % 2, :], slotb[:, 0:P]).then_inc(s_xsT, 1)
                elif what == "fin" and item[1] >= FC:
                    j = item[1] - FC
                    act.wait_ge(s_fin, units(b) + item[1] + 1)
                    act.wait_ge(s_scat, 16 * (tiles(b) + 1 + max(j - 2, 0)))
                    nc.scalar.activation(ys[:, j % 3, :], slotb[:, 0:D], ACT.Copy, scale=gates_now[:, j:j + 1]).then_inc(s_ys, 1)

            act.wait_ge(s_gwT, 1)
            nc.scalar.copy(wside[:, 0:EXPERTS], acc[:, 0:EXPERTS]).then_inc(s_gwTs, 1)
            act.wait_ge(s_wprod, 1)
            nc.scalar.copy(wdownT[:], acc[:, 0:P]).then_inc(s_wsave, 1)
            act.wait_ge(s_wprod, 2)
            nc.scalar.copy(wxq[:], acc[:, 0:P])
            nc.scalar.copy(wside[:, EXPERTS:SIDE], acc[:, P:P + 2 * HD]).then_inc(s_wsave, 1)
            for c in range(B + 1):
                if c == 2:
                    do(0, FIRST, QUERY)
                if c < B:
                    act.wait_ge(s_turn, c + 1)
                    nc.scalar.copy(xnT[:, c * T:(c + 1) * T], (gb, ub)[c % 2][:]).then_inc(s_xnT, 1)
                if c:
                    act.wait_ge(s_logits, c)
                    nc.scalar.copy(side[:, TB * (c - 1):TB * c, :].rearrange("p t e -> p (t e)"),
                                   ring[:, 2 + (c - 1) % 2, 0:TB * SIDE]).then_inc(s_side, 1)

            def sequence(b, kind):
                for item in scalar_items[kind]:
                    if not (kind == FIRST and item == QUERY):
                        do(b, kind, item)

            sequences(act, sequence)

        @block.vector
        def _(dve):
            count = {"local": 0, "base": 0}

            def link(ins):
                count["local"] += 1
                ins.then_inc(s_dve, 1)
                dve.wait_ge(s_dve, count["base"] + count["local"])

            def filled(b, kind, item):
                dve.wait_ge(s_misc, turns(b, kind, item))

            def by_token(ap):
                return ap.rearrange("p (t e) -> p t e", e=EXPERTS)

            def by_expert(ap):
                return ap.rearrange("p (e t) -> p e t", e=EXPERTS)

            def spread(ap, n):
                return ap.unsqueeze(2).broadcast_to([ap.shape[0], ap.shape[1], n])

            def tt(o, a, c, op):
                return nc.vector.tensor_tensor(o, a, c, op)

            def choose():
                dve.wait_ge(s_side, B)
                logits = side[:, :, 0:EXPERTS]
                link(nc.vector.tensor_reduce(lmax[:], logits, AX.X, ALU.max))
                link(tt(by_token(lshift), logits, spread(lmax[:], EXPERTS), ALU.subtract))
                dve.sem_inc(s_lread, 1)
                link(nc.vector.tensor_scalar(by_token(weight), count_f[:, 0:EXPERTS].unsqueeze(1).broadcast_to([P, NT, EXPERTS]),
                                             -1.0, float(EXPERTS), ALU.mult, ALU.add))
                dve.wait_ge(s_lexp, 1)
                link(nc.vector.tensor_reduce(lmax[:], by_token(lexp), AX.X, ALU.add))
                link(nc.vector.reciprocal(linv[:], lmax[:]))
                link(tt(by_token(probs), by_token(lexp), spread(linv[:], EXPERTS), ALU.mult))
                for k, (of, chosen) in enumerate(((probs, first), (probs2, second))):
                    link(nc.vector.tensor_reduce(best[:, k, :], by_token(of), AX.X, ALU.max))
                    link(tt(by_token(same), by_token(of), spread(best[:, k, :], EXPERTS), ALU.is_equal))
                    link(tt(same, same, weight, ALU.mult))
                    link(nc.vector.tensor_reduce(rank1[:], by_token(same), AX.X, ALU.max))
                    link(tt(by_token(chosen), by_token(weight), spread(rank1[:], EXPERTS), ALU.is_equal))
                    if k == 0:
                        link(nc.vector.scalar_tensor_tensor(out=probs2, in0=first, scalar=-2.0, in1=probs, op0=ALU.mult,
                                                            op1=ALU.add))
                tt(by_expert(mask16).rearrange("p e t -> p t e"), by_token(first), by_token(second), ALU.add).then_inc(s_mask, 1)

            def place():
                numbers = count_f[:, 0:NT].unsqueeze(1).broadcast_to([P, EXPERTS, NT])
                link(nc.vector.tensor_scalar(by_expert(restart), numbers, 0.0, None, ALU.is_gt))
                link(nc.vector.tensor_scalar(by_expert(thresh), numbers, float(P), None, ALU.mult))
                dve.wait_ge(s_prefix, 1)
                within, total = slotb[:, 0:NE], slotb[:, NE:2 * NE]
                link(nc.vector.tensor_tensor_scan(out=cumul, data0=restart, data1=total, initial=0.0, op0=ALU.mult, op1=ALU.add))
                link(tt(rank, cumul, total, ALU.subtract))
                link(tt(rank, rank, within, ALU.add))
                dve.sem_inc(s_spare, 1)
                link(tt(by_expert(same), spread(by_expert(cumul)[:, :, NT - 1], NT), by_expert(thresh), ALU.is_gt))
                link(nc.vector.tensor_reduce(tiles_of[:], by_expert(same), AX.X, ALU.add))
                link(nc.vector.tensor_tensor_scan(out=tile_end[:], data0=restart[:, 1:1 + EXPERTS], data1=tiles_of[:],
                                                  initial=0.0, op0=ALU.mult, op1=ALU.add))
                link(tt(tile_begin[:], tile_end[:], tiles_of[:], ALU.subtract))
                link(nc.vector.scalar_tensor_tensor(out=by_expert(rank), in0=spread(tile_begin[:], NT), scalar=float(P),
                                                    in1=by_expert(rank), op0=ALU.mult, op1=ALU.add))
                for k, chosen in enumerate((first, second)):
                    link(tt(by_token(picked), by_token(chosen), by_expert(rank).rearrange("p e t -> p t e"), ALU.mult))
                    link(nc.vector.tensor_reduce(slot_f[:, k, :], by_token(picked), AX.X, ALU.add))
                link(nc.vector.tensor_copy(slot_i[:], slot_f[:]))
                link(nc.vector.tensor_scalar(row_i[:], slot_i[:], P - 1, None, ALU.bitwise_and))
                link(nc.vector.tensor_copy(row_f[:], row_i[:]))
                link(tt(col_f[:], slot_f[:], row_f[:], ALU.subtract))
                link(nc.vector.tensor_scalar(col_f[:], col_f[:], 1.0 / P, None, ALU.mult))
                flat = payload[:].rearrange("p k t c -> p (k t) c")
                link(nc.vector.tensor_scalar(gate_f[:], best[:], ROUTED, None, ALU.mult))
                nc.vector.tensor_scalar(flat[:, :, 0], spread_lane(TOPK * NT), 0.0, None, ALU.add)
                for k in range(TOPK):
                    nc.vector.tensor_copy(payload[:, k, :, 1], count_f[:, 0:NT])
                nc.vector.memset(flat[:, :, 2], 1.0)
                gflat = gate_f[:].rearrange("p k t -> p (k t)")
                for c in range(PARTS):
                    link(nc.vector.tensor_copy(flat[:, :, 3 + c], gflat))
                    if c < PARTS - 1:
                        link(tt(gflat, gflat, flat[:, :, 3 + c], ALU.subtract))
                g3 = grid.rearrange("p (j e) -> p j e", e=EXPERTS)
                link(tt(g3, spread(count_f[0:1, 0:TILES], EXPERTS),
                        tile_end[0:1, :].unsqueeze(1).broadcast_to([1, TILES, EXPERTS]), ALU.is_ge))
                link(nc.vector.tensor_reduce(experts_f[:], g3, AX.X, ALU.add))
                link(nc.vector.tensor_scalar(experts_f[:], experts_f[:], float(EXPERTS - 1), None, ALU.min))
                link(nc.vector.tensor_copy(experts[:], experts_f[:]))
                dve.sem_inc(s_place, 1)

            def spread_lane(n):
                return lane[:].broadcast_to([P, n])

            def hot(i):
                if i >= DEEP:
                    dve.wait_ge(s_slot, i - DEEP + 1)
                for k in range(TOPK):
                    ins = nc.vector.tensor_scalar(col_hot[:, i % DEEP, k, :], count_f[:, 0:TILES], col_f[:, k, i:i + 1], None,
                                                  ALU.is_equal)
                ins.then_inc(s_hot, 1)
                for k in range(TOPK):
                    nc.vector.tensor_scalar(row_hot[:, i % DEEP, k, :], count_f[:], row_f[:, k, i:i + 1], None, ALU.is_equal)
                dve.wait_ge(s_hot, i + 1)
                tt(loaded[:, i % DEEP, 0], col_hot[:, i % DEEP, 0, :].unsqueeze(1).broadcast_to([P, PAYLOAD, TILES]),
                   spread(payload[:, 0, i, :], TILES), ALU.mult).then_inc(s_made, 1)

            def table():
                dve.wait_ge(s_slot, NT)
                found = found_room[:]
                link(nc.vector.tensor_copy(found, slotb[:, 0:PAYLOAD * TILES]))
                dve.sem_inc(s_ys, 1)
                col = found.rearrange("p (c n) -> p c n", c=PAYLOAD)
                link(nc.vector.scalar_tensor_tensor(out=col[:, 0], in0=col[:, 1], scalar=float(P), in1=col[:, 0],
                                                    op0=ALU.mult, op1=ALU.add))
                link(nc.vector.tensor_scalar(col[:, 2], col[:, 2], pad_minus[:], pad_row[:], ALU.mult, ALU.add))
                link(tt(col[:, 0], col[:, 0], col[:, 2], ALU.add))
                link(nc.vector.tensor_copy(ids[:], col[:, 0]))
                link(tt(col[:, 3], col[:, 3], col[:, 4], ALU.add))
                link(tt(gates[:], col[:, 3], col[:, 5], ALU.add))
                dve.sem_inc(s_table, 1)

            def do(b, kind, item):
                what = item[0]
                if what == "choose":
                    choose()
                elif what == "place":
                    place()
                elif what == "hot":
                    hot(item[1])
                elif what == "table":
                    table()
                elif what == "ids":
                    dve.wait_ge(s_scat, 16 * (tiles(b) + 1))
                    n = SHARE[kind]
                    nc.vector.tensor_copy(ids_now[:, 0:n], ids[:, bass.ds(tiles(b), n)])
                    nc.vector.tensor_copy(gates_now[:, 0:n], gates[:, bass.ds(tiles(b), n)]).then_inc(s_ids, 1)
                elif what == "query":
                    dve.wait_ge(s_q1, b + 1)
                    link(tt(qleft[:], bank_of(kind, item), qparts[:, 0, :], ALU.subtract))
                    dve.sem_inc(s_qread, 1)
                    link(nc.vector.tensor_copy(qparts[:, 1, :], qleft[:]))
                    tt(qparts[:, 2, :], qleft[:], qparts[:, 1, :], ALU.subtract).then_inc(s_q, 1)
                elif what == "keys":
                    if kind == FIRST:
                        dve.wait_ge(s_side, 1)
                    else:
                        dve.wait_ge(s_pv, GROUPS * b)
                        dve.wait_ge(s_kst, b)
                    kv = side[:, bass.ds(b * TB, TB), EXPERTS:SIDE]
                    nc.vector.tensor_copy(vaug[:, :, 0:HD], kv[:, :, HD:2 * HD])
                    link(nc.vector.tensor_copy(krows[:, :, 0:HD], kv[:, :, 0:HD]))
                    link(tt(kleft[:], kv[:, :, 0:HD], krows[:, :, 0:HD], ALU.subtract))
                    link(nc.vector.tensor_copy(krows[:, :, HD:2 * HD], kleft[:]))
                    link(tt(krows[:, :, 2 * HD:3 * HD], kleft[:], krows[:, :, HD:2 * HD], ALU.subtract))
                    nc.vector.tensor_copy(krows[:, :, 24:48], krows[:, :, 0:24])
                    nc.vector.tensor_copy(krows[:, :, 48:72], krows[:, :, 0:24]).then_inc(s_krows, 1)
                elif what == "a":
                    _, g, i = item
                    t, h0, n = A_BANKS[i]
                    dve.wait_ge(s_a, A_ALL * b + NA * g + i + 1)
                    keys = (t + 1) * P
                    nc.vector.tensor_reduce(nmax[:, t, HG * g + h0:HG * g + h0 + n],
                                            bank_of(kind, item)[:, 0:n * keys].rearrange("p (h s) -> p h s", h=n), AX.X,
                                            ALU.max, negate=True).then_inc(s_amax, 1)
                elif what == "split":
                    g = item[1]
                    m = nmax[:, :, HG * g:HG * g + HG]
                    dve.wait_ge(s_amax, A_ALL * b + NA * (g + 1))
                    if kind != FIRST or g:
                        dve.wait_ge(s_mT, GROUPS * b + g)
                    link(nc.vector.tensor_copy(mparts[:, :, 0, :], m))
                    link(tt(mleft[:], m, mparts[:, :, 0, :], ALU.subtract))
                    link(nc.vector.tensor_copy(mparts[:, :, 1, :], mleft[:]))
                    tt(mparts[:, :, 2, :], mleft[:], mparts[:, :, 1, :], ALU.subtract).then_inc(s_mparts, 1)
                elif what == "maxima":
                    g = item[1]
                    filled(b, kind, item)
                    if kind != FIRST or g:
                        dve.wait_ge(s_mst, 16 * (GROUPS * b + g))
                    link(nc.vector.tensor_copy(mT[:], bank16(kind, item)[0:PARTS * HG, 0:T]))
                    dve.sem_inc(s_mT, 1)
                elif what == "heads":
                    g = item[1]
                    filled(b, kind, item)
                    sums = bank_of(kind, item).rearrange("p (n r) -> p n r", r=32)
                    link(nc.vector.reciprocal(dinv[:], sums[:, :, HD]))
                    inverse = dinv[:].rearrange("p (t h) -> p t h", t=TB).unsqueeze(3).broadcast_to([P, TB, HG, HD])
                    link(tt(y[:, :, 32 * g:32 * g + 32].rearrange("p t (h d) -> p t h d", d=HD),
                            sums[:, :, 0:HD].rearrange("p (t h) d -> p t h d", t=TB), inverse, ALU.mult))
                    dve.sem_inc(s_y, 1)
                elif what == "u":
                    n = item[1]
                    if kind != FIRST or n:
                        dve.wait_ge(s_h, units(b) + n)
                    dve.wait_ge(s_th, units(b) + n + 1)
                    nc.vector.scalar_tensor_tensor(out=ga[:], in0=th[:, n % 2, :], scalar=1.0, in1=gb[:], op0=ALU.add,
                                                   op1=ALU.mult).then_inc(s_gfree, 1)
                elif what == "mul":
                    n = item[1]
                    dve.wait_ge(s_u, units(b) + n + 1)
                    dve.wait_ge(s_gfree, units(b) + n + 1)
                    if kind != FIRST or n >= 2:
                        dve.wait_ge(s_fin, units(b) + max(n - 1, 0))
                    scale = SHARED if n < FC else 1.0
                    nc.vector.scalar_tensor_tensor(out=hid[:, n % 2, :], in0=ga[:], scalar=scale, in1=ub[:], op0=ALU.mult,
                                                   op1=ALU.mult).then_inc(s_h, 1)
                elif what == "merge":
                    c = item[1]
                    dve.wait_ge(s_rl[c], 16)
                    rows = x_all[:, TB * c:TB * c + TB, :].rearrange("p t d -> p (t d)")
                    tt(rows, rows, rbuf(c), ALU.add).then_inc(s_merged, 1)
                elif what == "out":
                    dve.wait_ge(s_accfull, b + 1)
                    rows = x_all[:, bass.ds(b * TB, TB), :].rearrange("p t d -> p (t d)")
                    if kind == LAST:
                        dve.wait_ge(s_merged, B)
                    tt(rows, rows, acc[:], ALU.add).then_inc(s_res, 1)

            def sequence(b, kind):
                count["base"] = before(b, links[FIRST], links[MID]) + links["ahead"]
                count["local"] = 0
                for item in vector_items[kind]:
                    do(b, kind, item)
                assert count["local"] == links[kind], (kind, count["local"])

            each = {"choose": 17, "place": 29, "table": 7, "query": 2, "keys": 4, "split": 3, "maxima": 1, "heads": 2}
            links = {kind: sum(each.get(i[0], 0) for i in items[kind]) for kind in items}

            def moments(c):
                dve.wait_ge(s_xl[c], 16)
                for t in range(TB * c, TB * c + TB):
                    last = nc.vector.bn_stats(stats[:, t, :], x_all[:, t, :])
                link(last)
                for t in range(TB * c, TB * c + TB):
                    last = nc.vector.bn_aggr(meanvar[:, t, :], stats[:, t, :])
                link(last)
                nc.vector.tensor_scalar(vareps[:, TB * c:TB * c + TB], meanvar[:, TB * c:TB * c + TB, 1], EPS, None,
                                        ALU.add).then_inc(s_vareps, 1)

            def norm(c):
                dve.wait_ge(s_rstd, c // 2 + 1)
                for t in range(TB * c, TB * c + TB):
                    last = nc.vector.tensor_scalar(xn[:, t, :], x_all[:, t, :], meanvar[:, t, 0:1], rstd[:, t:t + 1],
                                                   ALU.subtract, ALU.mult)
                last.then_inc(s_norm, 1)

            for c in range(B + 2):
                if c < B:
                    moments(c)
                if c >= 2:
                    norm(c - 2)
            dve.wait_ge(s_const, 1)
            nc.vector.tensor_copy(count_f[:], count_i[:])
            link(nc.vector.tensor_copy(lane[:], lane_i[:]))
            link(nc.vector.tensor_scalar(pad_row[:], lane[:], float(PAD), None, ALU.add))
            link(nc.vector.tensor_scalar(pad_minus[:], pad_row[:], -1.0, None, ALU.mult))
            links["ahead"] = count["local"]
            sequences(dve, sequence)

        @block.gpsimd
        def _(pool):
            nc.gpsimd.memset(minus_half[:], -0.5)
            nc.gpsimd.memset(ident[:], 0.0).then_inc(s_made0, 1)
            for t in (wdown, wq, wkv, zeros):
                last = nc.gpsimd.memset(t[:], 0.0)
            last.then_inc(s_zero, 1)
            pool.wait_ge(s_made0, 1)
            nc.gpsimd.affine_select(out=ident[:], in_=ident[:], compare_op=ALU.not_equal, fill=1.0, base=0,
                                    pattern=[[-1, P]], channel_multiplier=1).then_inc(s_ident, 1)

            def power(c):
                pool.wait_ge(s_vareps, c + 2)
                both = slice(TB * c, TB * (c + 2))
                nc.gpsimd.tensor_tensor(rstd[:, both], vareps[:, both], minus_half[:, both], ALU.pow).then_inc(s_rstd, 1)

            power(0)
            for t in (never, krows, vaug):
                nc.gpsimd.memset(t[:], 0.0)
            power(2)
            nc.gpsimd.memset(earlier[:], 1.0)
            nc.gpsimd.memset(ones16[:], 1.0).then_inc(s_made0, 1)
            power(4)
            nc.gpsimd.iota(count_i[:], pattern=[[1, P]], base=0, channel_multiplier=0)
            nc.gpsimd.iota(lane_i[:], pattern=[[0, 1]], base=0, channel_multiplier=1)
            power(6)
            pool.wait_ge(s_made0, 2)
            nc.gpsimd.affine_select(out=never[:], in_=never[:], compare_op=ALU.is_ge, fill=NEVER, base=0,
                                    pattern=[[-1, P]], channel_multiplier=1)
            nc.gpsimd.affine_select(out=earlier[:], in_=earlier[:], compare_op=ALU.is_gt, fill=0.0, base=0,
                                    pattern=[[1, P]], channel_multiplier=-1)
            nc.gpsimd.memset(krows[:, :, MROW:STACKED], 1.0)
            nc.gpsimd.memset(vaug[:, :, HD:HD + 1], 1.0)
            pool.wait_ge(s_ident, 1)
            nc.gpsimd.tensor_copy(ident16[:], ident[:]).then_inc(s_const, 1)
            nc.gpsimd.memset(qst[:].rearrange("p h t -> p (h t)").bitcast(F32), 0.0).then_inc(s_zero, 1)
            rows = r_dram.rearrange("(p r) d -> p r d", p=P)
            pool.dma_start(rows, zeros[:].unsqueeze(1).broadcast_to([P, (N + P) // P, P])).then_inc(s_scat, 16)

            def gather(b, j):
                nc.gpsimd.indirect_dma_start(xs[:, j % 3, :], None, xn_dram,
                                             bass.IndirectOffsetOnAxis(ids_now[:, j:j + 1], 0)).then_inc(s_xs[j % 3], 16)

            def do(b, kind, item):
                what = item[0]
                if what == "hot":
                    i = item[1]
                    pool.wait_ge(s_hot, i + 1)
                    nc.gpsimd.tensor_tensor(loaded[:, i % DEEP, 1], col_hot[:, i % DEEP, 1, :].unsqueeze(1).broadcast_to([P, PAYLOAD, TILES]),
                                            payload[:, 1, i, :].unsqueeze(2).broadcast_to([P, PAYLOAD, TILES]),
                                            ALU.mult).then_inc(s_madep, 1)
                elif what == "ids":
                    pool.wait_ge(s_ids, b)
                    pool.sem_inc(s_apart, 1)
                    for j in range(3):
                        gather(b, j)
                elif what == "xs":
                    j = item[1] - FC
                    if j + 3 < SHARE[kind]:
                        pool.wait_ge(s_xsT, tiles(b) + j + 1)
                        pool.sem_inc(s_apart, 1)
                        gather(b, j + 3)
                elif what == "fin" and item[1] >= FC:
                    j = item[1] - FC
                    pool.wait_ge(s_ys, tiles(b) + j + 2)
                    pool.sem_inc(s_apart, 1)
                    pool.wait_ge(s_scat, 16 * (tiles(b) + j + 1))
                    pool.sem_inc(s_apart, 1)
                    nc.gpsimd.indirect_dma_start(r_dram, bass.IndirectOffsetOnAxis(ids_now[:, j:j + 1], 0), ys[:, j % 3, :],
                                                 None, compute_op=ALU.add).then_inc(s_scat, 16)

            def sequence(b, kind):
                for item in items[kind]:
                    do(b, kind, item)
                if kind == FIRST:
                    pool.wait_ge(s_xnst, 16 * (B + 1))

            sequences(pool, sequence)


_INS = ["L0_attn_x", "L0_attn_Wc_down", "L0_attn_Wq_up", "L0_attn_Wkv_up", "L0_attn_Wc_proj", "L0_ffn_gate_W",
        "L0_ffn_w1_e", "L0_ffn_w3_e", "L0_ffn_w2_e", "L0_ffn_w1_s", "L0_ffn_w3_s", "L0_ffn_w2_s"]


def kernel(**inputs):
    import numpy as _np
    import concourse.bacc as _bacc
    from concourse.bass_utils import run_bass_kernel_spmd as _run

    nc = _bacc.Bacc("TRN2", target_bir_lowering=False, num_devices=1)
    arrays, args = {}, []
    for name in _INS:
        a = _np.ascontiguousarray(inputs[name])
        arrays[f"in_{name}"] = a
        args.append(nc.dram_tensor(f"in_{name}", a.shape, mybir.dt.from_np(a.dtype), kind="ExternalInput").ap())
    shape = arrays["in_L0_attn_x"].shape
    args.append(nc.dram_tensor("out_0", shape, F32, kind="ExternalOutput").ap())
    build(nc, *args)
    r = _run(nc, [arrays], core_ids=[0])
    return r.results[0]["out_0"]
```
